# Optimizing a Trainium2 kernel written in Bass

```python
import numpy as np
import jax
import jax.numpy as jnp

def _softmax(x, axis=-1):
    return jax.nn.softmax(x, axis=axis)

def _gelu(x):
    return jax.nn.gelu(x, approximate=True)

def _silu(x):
    return jax.nn.silu(x)

def _sigmoid(x):
    return jax.nn.sigmoid(x)

def _layernorm(x, axis=-1, eps=1e-05):
    m = jnp.mean(x, axis=axis, keepdims=True)
    v = jnp.var(x, axis=axis, keepdims=True)
    return (x - m) / jnp.sqrt(v + eps)

def _scatter_add(tgt, idx, src, axis=0):
    return tgt.at[idx].add(src)

def _segment_sum(src, seg, n):
    return jax.ops.segment_sum(src, seg, n)
kernel_name = 'mk_xattn_seq_d1_seqx_r8_47dd1f'

def setup_inputs(seed: int=0):
    np.random.seed(seed)
    _w = jnp.asarray

    def _rec_inputs():
        import jax
        import jax.numpy as jnp
        _rk = jax.random.key(seed)
        x = 7.22e-05 + 1 * jax.random.normal(jax.random.fold_in(_rk, 1), (128, 64, 128), jnp.float32)
        _lenS = 64 - jax.random.randint(jax.random.fold_in(_rk, 7), (128,), 0, max(1, 64 // 4) + 1, jnp.int32)
        _lenS2 = 64 - jax.random.randint(jax.random.fold_in(_rk, 8), (128,), 0, max(1, 64 // 4) + 1, jnp.int32)
        _ctx_1024P = jax.random.normal(jax.random.fold_in(_rk, 11), (128, 16, 128), jnp.float32)
        _ctx_1024c = jax.random.dirichlet(jax.random.fold_in(_rk, 511), 0.3 * jnp.ones((16,), jnp.float32), (128, 64))
        _ctx_1024t = jnp.einsum('bsk,bkd->bsd', _ctx_1024c, _ctx_1024P)
        _ctx_1024t = _ctx_1024t * jax.lax.rsqrt(jnp.mean(jnp.square(_ctx_1024t)) + 1e-12) * 0.953939
        ctx_1024 = 4.13588e-05 + 0.999923 * (_ctx_1024t + 0.3 * jax.random.normal(jax.random.fold_in(_rk, 611), (128, 64, 128), jnp.float32))
        return (x, ctx_1024)
    x, ctx_1024 = _rec_inputs()

    def _L0_xattn_setup():
        import jax, jax.numpy as jnp
        import numpy as np
        import math
        NEG = -1e+32
        B, S, D, H, DFF, L = (16, 64, 128, 8, 512, 3)
        DK = D // H

        def layernorm(x, g, b, eps=1e-05):
            mu = x.mean(-1, keepdims=True)
            var = ((x - mu) ** 2).mean(-1, keepdims=True)
            return (x - mu) / jnp.sqrt(var + eps) * g + b

        def gen_dam(alphas, E, bmask):
            Hh, Ss, _ = alphas.shape
            g = -jnp.log(E + 1e-05)
            y_soft = jax.nn.softmax(alphas + g, axis=-1)
            idx = jnp.argmax(y_soft, axis=-1)
            y_hard = jax.nn.one_hot(idx, 2, dtype=y_soft.dtype)
            m = y_hard - jax.lax.stop_gradient(y_soft) + y_soft
            m = jnp.broadcast_to(m[:, :, 0:1], (Hh, Ss, Ss))
            m = jnp.triu(m)
            m = jnp.rot90(m, 1, axes=(1, 2))
            i = jnp.arange(Ss)[:, None]
            j = jnp.arange(Ss)[None, :]
            src = jnp.clip(j - i, 0, Ss - 1)
            shifted = m[:, jnp.arange(Ss)[:, None], src]
            mask_tri = jnp.where(j >= i, shifted, 0.0)
            masks = mask_tri + jnp.swapaxes(jnp.triu(mask_tri, 1), 1, 2)
            masks = jnp.triu(masks, bmask)
            return masks

        def attention(q, k, v, src_mask, dam, zero_pad, gammas):
            dk = q.shape[-1]
            Ss = q.shape[2]
            scores = jnp.einsum('bhqd,bhkd->bhqk', q, k) / math.sqrt(dk)
            damb = dam[None]
            smb = src_mask[None, None]
            sc = jnp.where(damb, scores, NEG)
            sc = jax.nn.softmax(sc, axis=-1)
            sc = sc * smb.astype(sc.dtype) * damb.astype(sc.dtype)
            distcum = jnp.cumsum(sc, axis=-1)
            disttot = jnp.sum(sc, axis=-1, keepdims=True)
            pos = jnp.abs(jnp.arange(Ss)[None, :] - jnp.arange(Ss)[:, None]).astype(scores.dtype)
            dist = jnp.sqrt(jnp.clip((disttot - distcum) * pos[None, None], 0.0, None))
            dist = jax.lax.stop_gradient(dist)
            gamma = -jax.nn.softplus(gammas)[None]
            te = jnp.clip(jnp.exp(dist * gamma), 1e-05, 100000.0)
            scores = scores * te
            scores = jnp.where(smb, scores, NEG)
            scores = jnp.where(damb, scores, NEG)
            scores = jax.nn.softmax(scores, axis=-1)
            if zero_pad:
                scores = scores.at[:, :, 0, :].set(0.0)
            return jnp.einsum('bhqk,bhkd->bhqd', scores, v)

        def transformer_layer(bmask, query, key, values, apply_pos, p):
            Bb, Ss, Dd = query.shape
            Hh = p['gammas'].shape[0]
            dam = gen_dam(p['alphas'], p['E'], bmask) == 0
            src_mask = jnp.triu(jnp.ones((Ss, Ss), jnp.int32), bmask) == 0
            k = (key @ p['kW'].T + p['kb']).reshape(Bb, Ss, Hh, -1).transpose(0, 2, 1, 3)
            q = (query @ p['kW'].T + p['kb']).reshape(Bb, Ss, Hh, -1).transpose(0, 2, 1, 3)
            v = (values @ p['vW'].T + p['vb']).reshape(Bb, Ss, Hh, -1).transpose(0, 2, 1, 3)
            att = attention(q, k, v, src_mask, dam, bmask == 0, p['gammas'])
            concat = att.transpose(0, 2, 1, 3).reshape(Bb, Ss, Dd)
            q2 = concat @ p['oW'].T + p['ob']
            x = layernorm(query + q2, p['ln1_g'], p['ln1_b'])
            if apply_pos:
                ff = jax.nn.relu(x @ p['w1'].T + p['b1']) @ p['w2'].T + p['b2']
                x = layernorm(x + ff, p['ln2_g'], p['ln2_b'])
            return x
        key = jax.random.key(seed)
        ks = jax.random.split(key, 16)
        sc = 0.02
        return {'q_embed_data': jax.random.normal(ks[0], (B, S, D), jnp.float32), 'qa_embed_data': jax.random.normal(ks[1], (B, S, D), jnp.float32), 'kW': sc * jax.random.normal(ks[2], (L, D, D), jnp.float32), 'kb': jnp.zeros((L, D), jnp.float32), 'vW': sc * jax.random.normal(ks[3], (L, D, D), jnp.float32), 'vb': jnp.zeros((L, D), jnp.float32), 'oW': sc * jax.random.normal(ks[4], (L, D, D), jnp.float32), 'ob': jnp.zeros((L, D), jnp.float32), 'gammas': 0.5 * jax.random.normal(ks[5], (L, H, 1, 1), jnp.float32), 'alphas': 0.001 * jax.random.normal(ks[6], (L, H, S, 2), jnp.float32), 'ln1_g': jnp.ones((L, D), jnp.float32), 'ln1_b': jnp.zeros((L, D), jnp.float32), 'w1': sc * jax.random.normal(ks[7], (L, DFF, D), jnp.float32), 'b1': jnp.zeros((L, DFF), jnp.float32), 'w2': sc * jax.random.normal(ks[8], (L, D, DFF), jnp.float32), 'b2': jnp.zeros((L, D), jnp.float32), 'ln2_g': jnp.ones((L, D), jnp.float32), 'ln2_b': jnp.zeros((L, D), jnp.float32), 'gumbel_E': jax.random.exponential(ks[9], (L, H, S, 2), jnp.float32)}
    _L0_xattn_all = _L0_xattn_setup()
    _L0_xattn_in = {k: v for k, v in _L0_xattn_all.items() if k in ('kW', 'kb', 'vW', 'vb', 'oW', 'ob', 'gammas', 'alphas', 'ln1_g', 'ln1_b', 'w1', 'b1', 'w2', 'b2', 'ln2_g', 'ln2_b', 'gumbel_E')}
    del _L0_xattn_all
    return {'x': x, 'ctx_1024': ctx_1024, 'L0_xattn_kW': _L0_xattn_in['kW'], 'L0_xattn_kb': _L0_xattn_in['kb'], 'L0_xattn_vW': _L0_xattn_in['vW'], 'L0_xattn_vb': _L0_xattn_in['vb'], 'L0_xattn_oW': _L0_xattn_in['oW'], 'L0_xattn_ob': _L0_xattn_in['ob'], 'L0_xattn_gammas': _L0_xattn_in['gammas'], 'L0_xattn_alphas': _L0_xattn_in['alphas'], 'L0_xattn_ln1_g': _L0_xattn_in['ln1_g'], 'L0_xattn_ln1_b': _L0_xattn_in['ln1_b'], 'L0_xattn_w1': _L0_xattn_in['w1'], 'L0_xattn_b1': _L0_xattn_in['b1'], 'L0_xattn_w2': _L0_xattn_in['w2'], 'L0_xattn_b2': _L0_xattn_in['b2'], 'L0_xattn_ln2_g': _L0_xattn_in['ln2_g'], 'L0_xattn_ln2_b': _L0_xattn_in['ln2_b'], 'L0_xattn_gumbel_E': _L0_xattn_in['gumbel_E']}

def reference(x, ctx_1024, L0_xattn_kW, L0_xattn_kb, L0_xattn_vW, L0_xattn_vb, L0_xattn_oW, L0_xattn_ob, L0_xattn_gammas, L0_xattn_alphas, L0_xattn_ln1_g, L0_xattn_ln1_b, L0_xattn_w1, L0_xattn_b1, L0_xattn_w2, L0_xattn_b2, L0_xattn_ln2_g, L0_xattn_ln2_b, L0_xattn_gumbel_E):
    import jax
    import jax.numpy as jnp

    def _L0_xattn_ref(q_embed_data, qa_embed_data, kW, kb, vW, vb, oW, ob, gammas, alphas, ln1_g, ln1_b, w1, b1, w2, b2, ln2_g, ln2_b, gumbel_E):
        import jax, jax.numpy as jnp
        import numpy as np
        import math
        NEG = -1e+32
        B, S, D, H, DFF, L = (16, 64, 128, 8, 512, 3)
        DK = D // H

        def layernorm(x, g, b, eps=1e-05):
            mu = x.mean(-1, keepdims=True)
            var = ((x - mu) ** 2).mean(-1, keepdims=True)
            return (x - mu) / jnp.sqrt(var + eps) * g + b

        def gen_dam(alphas, E, bmask):
            Hh, Ss, _ = alphas.shape
            g = -jnp.log(E + 1e-05)
            y_soft = jax.nn.softmax(alphas + g, axis=-1)
            idx = jnp.argmax(y_soft, axis=-1)
            y_hard = jax.nn.one_hot(idx, 2, dtype=y_soft.dtype)
            m = y_hard - jax.lax.stop_gradient(y_soft) + y_soft
            m = jnp.broadcast_to(m[:, :, 0:1], (Hh, Ss, Ss))
            m = jnp.triu(m)
            m = jnp.rot90(m, 1, axes=(1, 2))
            i = jnp.arange(Ss)[:, None]
            j = jnp.arange(Ss)[None, :]
            src = jnp.clip(j - i, 0, Ss - 1)
            shifted = m[:, jnp.arange(Ss)[:, None], src]
            mask_tri = jnp.where(j >= i, shifted, 0.0)
            masks = mask_tri + jnp.swapaxes(jnp.triu(mask_tri, 1), 1, 2)
            masks = jnp.triu(masks, bmask)
            return masks

        def attention(q, k, v, src_mask, dam, zero_pad, gammas):
            dk = q.shape[-1]
            Ss = q.shape[2]
            scores = jnp.einsum('bhqd,bhkd->bhqk', q, k) / math.sqrt(dk)
            damb = dam[None]
            smb = src_mask[None, None]
            sc = jnp.where(damb, scores, NEG)
            sc = jax.nn.softmax(sc, axis=-1)
            sc = sc * smb.astype(sc.dtype) * damb.astype(sc.dtype)
            distcum = jnp.cumsum(sc, axis=-1)
            disttot = jnp.sum(sc, axis=-1, keepdims=True)
            pos = jnp.abs(jnp.arange(Ss)[None, :] - jnp.arange(Ss)[:, None]).astype(scores.dtype)
            dist = jnp.sqrt(jnp.clip((disttot - distcum) * pos[None, None], 0.0, None))
            dist = jax.lax.stop_gradient(dist)
            gamma = -jax.nn.softplus(gammas)[None]
            te = jnp.clip(jnp.exp(dist * gamma), 1e-05, 100000.0)
            scores = scores * te
            scores = jnp.where(smb, scores, NEG)
            scores = jnp.where(damb, scores, NEG)
            scores = jax.nn.softmax(scores, axis=-1)
            if zero_pad:
                scores = scores.at[:, :, 0, :].set(0.0)
            return jnp.einsum('bhqk,bhkd->bhqd', scores, v)

        def transformer_layer(bmask, query, key, values, apply_pos, p):
            Bb, Ss, Dd = query.shape
            Hh = p['gammas'].shape[0]
            dam = gen_dam(p['alphas'], p['E'], bmask) == 0
            src_mask = jnp.triu(jnp.ones((Ss, Ss), jnp.int32), bmask) == 0
            k = (key @ p['kW'].T + p['kb']).reshape(Bb, Ss, Hh, -1).transpose(0, 2, 1, 3)
            q = (query @ p['kW'].T + p['kb']).reshape(Bb, Ss, Hh, -1).transpose(0, 2, 1, 3)
            v = (values @ p['vW'].T + p['vb']).reshape(Bb, Ss, Hh, -1).transpose(0, 2, 1, 3)
            att = attention(q, k, v, src_mask, dam, bmask == 0, p['gammas'])
            concat = att.transpose(0, 2, 1, 3).reshape(Bb, Ss, Dd)
            q2 = concat @ p['oW'].T + p['ob']
            x = layernorm(query + q2, p['ln1_g'], p['ln1_b'])
            if apply_pos:
                ff = jax.nn.relu(x @ p['w1'].T + p['b1']) @ p['w2'].T + p['b2']
                x = layernorm(x + ff, p['ln2_g'], p['ln2_b'])
            return x

        def P(l):
            return {'kW': kW[l], 'kb': kb[l], 'vW': vW[l], 'vb': vb[l], 'oW': oW[l], 'ob': ob[l], 'gammas': gammas[l], 'alphas': alphas[l], 'ln1_g': ln1_g[l], 'ln1_b': ln1_b[l], 'w1': w1[l], 'b1': b1[l], 'w2': w2[l], 'b2': b2[l], 'ln2_g': ln2_g[l], 'ln2_b': ln2_b[l], 'E': gumbel_E[l]}
        y = transformer_layer(1, qa_embed_data, qa_embed_data, qa_embed_data, True, P(0))
        x = transformer_layer(1, q_embed_data, q_embed_data, q_embed_data, False, P(1))
        x = transformer_layer(0, x, x, y, True, P(2))
        return x
    x = _L0_xattn_ref(x, ctx_1024, L0_xattn_kW, L0_xattn_kb, L0_xattn_vW, L0_xattn_vb, L0_xattn_oW, L0_xattn_ob, L0_xattn_gammas, L0_xattn_alphas, L0_xattn_ln1_g, L0_xattn_ln1_b, L0_xattn_w1, L0_xattn_b1, L0_xattn_w2, L0_xattn_b2, L0_xattn_ln2_g, L0_xattn_ln2_b, L0_xattn_gumbel_E)
    return x

_drawn_inputs = setup_inputs


def setup_inputs(seed=0):
    import zlib

    import numpy as np

    out = dict(_drawn_inputs(seed))
    spreads = {'L0_xattn_kb': (0.0, 2.0),
     'L0_xattn_vb': (0.0, 0.1),
     'L0_xattn_ob': (0.0, 0.1),
     'L0_xattn_ln1_g': (1.0, 0.2),
     'L0_xattn_ln1_b': (0.0, 0.1),
     'L0_xattn_b1': (0.0, 0.271),
     'L0_xattn_b2': (0.0, 0.1),
     'L0_xattn_ln2_g': (1.0, 0.2),
     'L0_xattn_ln2_b': (0.0, 0.1)}
    factors = {'L0_xattn_kW': 8.0,
     'L0_xattn_gammas': 24.702,
     'L0_xattn_alphas': 64.0,
     'L0_xattn_gumbel_E': 38.27}
    for name, (base, spread) in spreads.items():
        noise = np.random.default_rng([zlib.crc32(name.encode()), seed]).standard_normal(out[name].shape)
        drawn = base * np.exp(spread * noise) if base else spread * noise
        out[name] = jnp.asarray(drawn.astype(out[name].dtype))
    for name, factor in factors.items():
        out[name] = (out[name] * factor).astype(out[name].dtype)
    return out
```

```python
from contextlib import ExitStack

import concourse.bass as bass
from concourse import mybir

ALU = mybir.AluOpType
ACT = mybir.ActivationFunctionType
AX_X = mybir.AxisListType.X
F32 = mybir.dt.float32
BF16 = mybir.dt.bfloat16

P = 128
B, S, D, H, DFF, L = 128, 64, 128, 8, 512, 3
DK = D // H
BT = P // S
TB = 4
GROUPS = B // (BT * TB)
TOK = TB * P
BB = BT * TB
HP = H // 2
VW = 2 * DK + 2
FC = DFF // P
STEPS = L * TB
NEG = -1e32
TINY = 1e-30
EPS_LN = 1e-5
EPS_LOG = 1e-5
TE_MIN = 1e-5
BMASK = (1, 1, 0)
SKEW = 2 * S

SCHEDULE = [
    [[("yT", 0, -1, 0), ("attT", 1, -1, 0)], [("proj", 1, -1, 0)]],
    [[("xT", 1, 0, 0)], [("key", 1, 0, 0)]],
    [[("value", 1, 0, 0)], []],
    [[("norm1", 1, -1, 0)], []],
    [[("attT", 2, -2, 0)], [("proj", 2, -2, 0), ("x1T", 1, -1, 0)]],
    [[("key", 2, -1, 0), ("norm1", 2, -2, 0)], [("x1T", 2, -2, 0)]],
    [[("ff1", 2, -2, 0), ("ff1", 2, -2, 1)], [("ff1", 2, -2, 2), ("ff1", 2, -2, 3), ("value", 2, -1, 0)]],
    [[("ff2", 2, -2, 0)], [("norm2", 2, -2, 0)]],
    [[("attT", 0, 0, 0)], [("proj", 0, 0, 0)]],
    [[("xT", 0, 1, 0), ("norm1", 0, 0, 0)], [("key", 0, 1, 0), ("x1T", 0, 0, 0)]],
    [[("ff1", 0, 0, 0), ("ff1", 0, 0, 1), ("value", 0, 1, 0)], [("ff1", 0, 0, 2), ("ff1", 0, 0, 3)]],
    [[("ff2", 0, 0, 0)], [("norm2", 0, 0, 0)]],
]
ORDER = [job for step in SCHEDULE for part in step for job in part]
FIRST_ROUND, LOOP_FROM, LOOP_TO, LAST_ROUND = -1, 2, GROUPS - 2, GROUPS + 1


def exists(i, c):
    return not isinstance(i, int) or 0 <= i + c < GROUPS


def line(i, a, b):
    return i * a + b


def block_no(i, layer, c):
    if isinstance(i, int):
        k = i + c
        return 2 * min(k + 2, GROUPS) + k if layer == 2 else 2 * k + max(k - 1, 0) + layer
    return line(i, 3, 3 * c + (4 if layer == 2 else layer - 1))


def tile_no(i, layer, c, t):
    if isinstance(i, int):
        return TB * block_no(i, layer, c) + t
    return line(i, 3 * TB, TB * (3 * c + (4 if layer == 2 else layer - 1)) + t)


def ffn_no(i, layer, c):
    if isinstance(i, int):
        k = i + c
        return min(k + 2, GROUPS) + k if layer == 2 else k + max(k - 1, 0)
    return line(i, 2, 2 * c + (2 if layer == 2 else -1))


def job_count(i, kind, layer, c, chunk=0):
    if kind == "ff1":
        if isinstance(i, int):
            return FC * ffn_no(i, layer, c) + chunk + 1
        return line(i, 2 * FC, FC * (2 * c + (2 if layer == 2 else -1)) + chunk + 1)
    if kind in ("ff2", "norm2"):
        return ffn_no(i, layer, c) + 1
    if kind == "xT":
        return line(i, 2, 2 * c + layer + 1)
    if kind == "yT":
        return line(i, 1, c + 1)
    return block_no(i, layer, c) + 1


def after(eng, sem, count):
    if not isinstance(count, int) or count > 0:
        eng.wait_ge(sem, count)


def at_step(r):
    d, r = divmod(r, STEPS)
    layer = r // TB
    return layer, d - (layer == 2), r % TB


def rounds(eng, step):
    for i in range(FIRST_ROUND, LOOP_FROM):
        for r in range(STEPS):
            step(i, r)
    with eng.Fori(LOOP_FROM, LOOP_TO) as i:
        for r in range(STEPS):
            step(i, r)
    for i in range(LOOP_TO, LAST_ROUND + 1):
        for r in range(STEPS):
            step(i, r)


def build(nc, x, ctx, kW, kb, vW, vb, oW, ob, gammas, alphas, ln1_g, ln1_b, w1, b1, w2, b2, ln2_g, ln2_b,
          gumbel, out):
    with ExitStack() as stack:
        def sb(name, shape, dt=F32):
            return stack.enter_context(nc.sbuf_tensor(name, shape, dt))

        def sem(name):
            return stack.enter_context(nc.semaphore(name))

        psS = [stack.enter_context(nc.psum_tensor(f"psS{n}", [P, TOK], F32)) for n in range(TB)]
        psT = stack.enter_context(nc.psum_tensor("psT", [P, TOK], F32))
        psO = stack.enter_context(nc.psum_tensor("psO", [P, TOK], F32))
        psJ = [stack.enter_context(nc.psum_tensor(f"psJ{n}", [P, TOK], F32)) for n in range(2)]

        identf = sb("identf", [P, P])
        identb = sb("identb", [P, P], BF16)
        mask_bias = sb("mask_bias", [P, L, H * S], BF16)
        causal_bias = sb("causal_bias", [P, 2, H * S], BF16)
        keep = sb("keep", [P, 2, H * S])
        decay = sb("decay", [P, L, H * S])
        kWT = sb("kWT", [P, L, D])
        vWT = sb("vWT", [P, L, D])
        oWT = sb("oWT", [P, L, D])
        w1T = sb("w1T", [P, 2, DFF])
        w2T = sb("w2T", [P, 2, FC, D])
        cols = sb("cols", [P, 8, L])
        HKB, VB, OB, G1, B1, BF2, G2, B2 = range(8)
        b1c = sb("b1c", [P, L, FC])
        vectors = sb("vectors", [(8 + FC) * L, D])
        g2row = sb("g2row", [P, D])
        b2row = sb("b2row", [P, D])
        small = sb("small", [P, 4])
        xin = sb("xin", [P, 2, TB, D])
        xT = sb("xT", [P, 2, TOK])
        x1T = sb("x1T", [P, TOK])
        xfT = sb("xfT", [P, TOK])
        yT = sb("yT", [P, TOK])
        kh = sb("kh", [P, L, TOK])
        kx = [sb(f"kx{n}", [P, H, TOK]) for n in range(L)]
        vx = [sb(f"vx{n}", [P, BB, HP, VW]) for n in range(L)]
        E = [sb(f"E{n}", [P, H * S + 1]) for n in range(TB)]
        W = [sb(f"W{n}", [P, H * S]) for n in range(TB)]
        PT = [sb(f"PT{n}", [P, HP, P]) for n in range(2)]
        tree = [sb(f"tree{n}", [P, H, n]) for n in (32, 16, 8, 4, 2)]
        neg1 = sb("neg1", [P, TB, H])
        den1 = sb("den1", [P, TB, H])
        rden1 = sb("rden1", [P, TB, H])
        neg2 = sb("neg2", [P, TB, H])
        rden2 = sb("rden2", [P, TB, HP, 2])
        att = sb("att", [P, L, TB, D])
        attT = sb("attT", [P, TOK])
        zT = sb("zT", [P, TOK])
        zn = sb("zn", [P, TB, D])
        stats = sb("stats", [P, TB, 6])
        mv = sb("mv", [P, TB, 4])
        mean = sb("mean", [P, TB])
        var4 = sb("var4", [P, TB])
        lvar = sb("lvar", [P, TB])
        rstd = sb("rstd", [P, TB])
        hT = sb("hT", [P, FC, TOK])
        rT = sb("rT", [P, TOK])
        rn = sb("rn", [P, TB, D])
        outb = sb("outb", [P, TB, D])
        flat0, flat1, flat2 = (k[:].rearrange("p h t -> p (h t)") for k in kx)
        n_nat, n_w = 3 * L * D, 2 * DFF
        natural = flat0[:, 0:n_nat].rearrange("p (n l d) -> p n l d", n=3, l=L)
        w1n = flat0[:, n_nat:n_nat + n_w].rearrange("p (n c d) -> p n c d", n=2, c=FC)
        w2n = flat0[:, n_nat + n_w:n_nat + 2 * n_w].rearrange("p (n f) -> p n f", n=2)
        al = flat1[:, 0:L * H * S * 2].rearrange("p (l h s c) -> p l h s c", l=L, h=H, c=2)
        ge = flat2[:, 0:L * H * S * 2].rearrange("p (l h s c) -> p l h s c", l=L, h=H, c=2)
        hidden = sb("hidden", [P, L, H, SKEW])
        shifted_mask = hT[:].rearrange("p c t -> p (c t)")[:, 0:L * H * S].rearrange("p (l h s) -> p l h s", l=L, h=H)
        gam = sb("gam", [P, 5, L * H])
        zeros = sb("zeros", [P, H * S])
        dist_ij = sb("dist_ij", [P, H * S])
        skew = nc.dram_tensor("skew", [L * H, S * (SKEW + 1)], F32, kind="Internal").ap()

        loaded = sem("loaded")
        weights_loaded = sem("weights_loaded")
        setup_pool = sem("setup_pool")
        setup_act = sem("setup_act")
        setup_dve = sem("setup_dve")
        skew_written = sem("skew_written")
        skew_read = sem("skew_read")
        wT_ready = sem("wT_ready")
        wT_done = sem("wT_done")
        scores_ready = sem("scores_ready")
        max1_done = sem("max1_done")
        shift1_done = sem("shift1_done")
        exp1_done = sem("exp1_done")
        causal_ready = sem("causal_ready")
        tree_step = sem("tree_step")
        rden1_done = sem("rden1_done")
        scan_done = sem("scan_done")
        decay_done = sem("decay_done")
        dist_done = sem("dist_done")
        log_done = sem("log_done")
        root_done = sem("root_done")
        te_done = sem("te_done")
        logits_done = sem("logits_done")
        max2_done = sem("max2_done")
        shift2_done = sem("shift2_done")
        logitsT_ready = sem("logitsT_ready")
        probs_done = sem("probs_done")
        weighted_ready = sem("weighted_ready")
        rden2_done = sem("rden2_done")
        att_done = sem("att_done")
        kinds = ("xT", "key", "value", "attT", "proj", "norm1", "x1T", "ff1", "ff2", "norm2", "yT")
        ready = {k: sem(f"{k}_ready") for k in kinds}
        done = {k: sem(f"{k}_done") for k in kinds}
        x_loaded = [sem(f"x_loaded{n}") for n in range(2)]
        kx_filled = [sem(f"kx_filled{n}") for n in range(L)]
        padded = sem("padded")
        stats_step = sem("stats_step")
        lvar_done = sem("lvar_done")
        rstd_done = sem("rstd_done")
        out_scaled = sem("out_scaled")
        out_done = sem("out_done")
        stored = sem("stored")

        x_groups = [a.rearrange("(s t b) q d -> s (b q) t d", t=TB, b=BT) for a in (ctx, x)]
        out_groups = out.rearrange("(s t b) q d -> s (b q) t d", t=TB, b=BT)

        def per_head(ap):
            return ap.rearrange("p (h k) -> p h k", h=H)

        def over_keys(ap):
            return ap.unsqueeze(2).to_broadcast([P, H, S])

        def norm_no(i, kind, layer, c):
            n = 0
            me = ORDER.index((kind, layer, -c and c or c, 0)) if (kind, layer, c, 0) in ORDER else None
            norms = [(j, job) for j, job in enumerate(ORDER) if job[0] in ("norm1", "norm2")]
            if isinstance(i, int):
                for past in range(FIRST_ROUND, i + 1):
                    for j, job in norms:
                        if exists(past, job[2]) and (past < i or j < me):
                            n += 1
                return n
            before = norm_no(LOOP_FROM, kind, layer, c)
            return line(i, len(norms), before - LOOP_FROM * len(norms))

        def bank_free(eng, i, job):
            n = ORDER.index(job) - 2
            j = 0
            while True:
                if n < 0:
                    n += len(ORDER) + (1 if len(ORDER) % 2 else 0)
                    if n >= len(ORDER):
                        n -= 2
                    j -= 1
                kind, layer, c, chunk = ORDER[n]
                if isinstance(i, int) and i + j < FIRST_ROUND:
                    return
                if exists(i, c + j):
                    count = job_count(i, kind, layer, c + j, chunk)
                    if kind == "value":
                        count = count * 2
                    after(eng, done[kind], count)
                    return
                n -= 2

        def bank(job):
            return psJ[ORDER.index(job) % 2]

        ffn = {0: 0, 2: 1}

        block = stack.enter_context(nc.Block())

        @block.sync
        def _(sp):
            sp.dma_start(al.rearrange("p l h s c -> p (l h s c)"),
                         alphas.rearrange("l h s c -> (l h s c)").partition_broadcast(P)).then_inc(loaded, 16)
            sp.dma_start(ge.rearrange("p l h s c -> p (l h s c)"),
                         gumbel.rearrange("l h s c -> (l h s c)").partition_broadcast(P)).then_inc(loaded, 16)
            sp.dma_start(gam[:, 0, :], gammas.rearrange("l h a b -> (l h a b)").partition_broadcast(P)).then_inc(loaded, 16)
            for n, a in enumerate((kW, vW, oW)):
                sp.dma_start(natural[:, n], a.rearrange("l o i -> o l i")).then_inc(weights_loaded, 16)
            for n, l in enumerate((0, 2)):
                sp.dma_start(w1n[:, n], w1[l].rearrange("(c p) i -> p c i", p=P)).then_inc(weights_loaded, 16)
                sp.dma_start(w2n[:, n], w2[l]).then_inc(weights_loaded, 16)
            for n, a in enumerate((kb, vb, ob, ln1_g, ln1_b, b2, ln2_g, ln2_b)):
                sp.dma_start(vectors[n * L:(n + 1) * L, :], a).then_inc(weights_loaded, 16)
            sp.dma_start(vectors[8 * L:, :], b1.rearrange("l (c p) -> (l c) p", p=P)).then_inc(weights_loaded, 16)
            sp.dma_start(g2row[:], ln2_g[L - 1].partition_broadcast(P)).then_inc(weights_loaded, 16)
            sp.dma_start(b2row[:], ln2_b[L - 1].partition_broadcast(P)).then_inc(weights_loaded, 16)
            sp.wait_ge(setup_dve, 3)
            sp.dma_start(bass.AP(skew.tensor, 0, [[SKEW + 1, S], [S * (SKEW + 1), L * H], [1, SKEW]]),
                         hidden[0:S].rearrange("p l h u -> p (l h) u")).then_inc(skew_written, 16)
            sp.wait_ge(skew_written, 16)
            for n in range(BT):
                sp.dma_start(shifted_mask[n * S:(n + 1) * S].rearrange("p l h k -> p (l h) k"),
                             bass.AP(skew.tensor, S, [[SKEW, S], [S * (SKEW + 1), L * H], [1, S]])).then_inc(skew_read, 16)

            def step(i, r):
                for part in SCHEDULE[r]:
                    for kind, layer, c, chunk in part:
                        if not exists(i, c):
                            continue
                        if kind == "xT":
                            k = c + 1
                            if exists(i, k):
                                sp.wait_ge(ready["xT"], job_count(i, "xT", layer, c))
                                src = x_groups[layer]
                                sp.dma_start(xin[:, layer], src[i + k]).then_inc(x_loaded[layer], 16)
                        if kind == "key":
                            sp.wait_ge(done["key"], job_count(i, "key", layer, c))
                            for h in range(H):
                                rows = slice(h * DK, (h + 1) * DK)
                                sp.dma_start(kx[layer][rows, h, :], kh[rows, layer, :]).then_inc(kx_filled[layer], 16)
                        if kind == "norm2" and layer == 2:
                            sp.wait_ge(out_done, line(i, 1, c + 1))
                            sp.dma_start(out_groups[i + c], outb[:]).then_inc(stored, 16)

            for layer in range(2):
                sp.dma_start(xin[:, layer], x_groups[layer][0]).then_inc(x_loaded[layer], 16)
            rounds(sp, step)
            sp.wait_ge(stored, 16 * GROUPS)

        @block.tensor
        def _(pe):
            def transposes(dst, parts, sem_):
                for n, src in enumerate(parts):
                    last = nc.tensor.transpose(dst[:, n * P:(n + 1) * P], src, identf[:])
                last.then_inc(sem_, 1)

            pe.wait_ge(setup_pool, 4)
            pe.wait_ge(weights_loaded, WEIGHT_LOADS * 16)
            rows = (8 + FC) * L
            nc.tensor.transpose(psT[:, 0:rows], vectors[:], identf[0:rows, 0:rows]).then_inc(wT_ready, 1)
            for n in range(3):
                transposes(psS[n], [natural[:, n, l, :] for l in range(L)], wT_ready)
            for n in range(2):
                if n:
                    pe.wait_ge(wT_done, 3)
                transposes(psS[3] if not n else psS[0], [w1n[:, n, c, :] for c in range(FC)], wT_ready)
            for n in range(2):
                pe.wait_ge(wT_done, n + 4)
                transposes(psS[n + 1], [w2n[:, n, c * P:(c + 1) * P] for c in range(FC)], wT_ready)
            pe.wait_ge(wT_done, 9)
            pe.wait_ge(setup_dve, SETUP_DVE)
            pe.wait_ge(setup_pool, SETUP_POOL)

            def scores(i, layer, c, t):
                n = tile_no(i, layer, c, t)
                after(pe, logits_done, n + 1 - TB)
                if t == 0:
                    pe.wait_ge(done["key"], job_count(i, "key", layer, c))
                    pe.wait_ge(kx_filled[layer], line(i, 16 * H, 16 * H * (c + 1)))
                nc.tensor.matmul(psS[t][:], identb[:], mask_bias[:, layer], start=True, stop=False, skip_group_check=True)
                for b in range(BT):
                    tok = slice((t * BT + b) * S, (t * BT + b + 1) * S)
                    last = nc.tensor.matmul(psS[t][b * S:(b + 1) * S, :], kh[:, layer, tok], kx[layer][:, :, tok],
                                            start=False, stop=True, skip_group_check=True)
                last.then_inc(scores_ready, 1)

            def causal(i, layer, c, t):
                n = tile_no(i, layer, c, t)
                pe.wait_ge(shift1_done, n + 1)
                nc.tensor.matmul(psS[t][:], identb[:], causal_bias[:, BMASK[layer]], start=False, stop=True,
                                 skip_group_check=True).then_inc(causal_ready, 1)

            def logitsT(i, layer, c, t):
                n = tile_no(i, layer, c, t)
                after(pe, probs_done, n)
                pe.wait_ge(shift2_done, n + 1)
                transposes(psT, [W[t][:, g * P:(g + 1) * P] for g in range(HP)], logitsT_ready)

            def weighted(i, layer, c, t):
                n = tile_no(i, layer, c, t)
                after(pe, att_done, n)
                if t == 0:
                    pe.wait_ge(done["value"], job_count(i, "value", layer, c) * 2)
                pe.wait_ge(probs_done, n + 1)
                for b in range(BT):
                    for g in range(HP):
                        last = nc.tensor.matmul(psO[b * S:(b + 1) * S, g * VW:(g + 1) * VW],
                                                PT[t % 2][:, g, b * S:(b + 1) * S], vx[layer][:, t * BT + b, g, :],
                                                start=True, stop=True)
                last.then_inc(weighted_ready, 1)

            def job(i, kind, layer, c, chunk):
                me = (kind, layer, c, chunk)
                dst = bank(me)
                bank_free(pe, i, me)
                count = lambda k, l=layer, cc=c: job_count(i, k, l, cc)
                if kind == "xT":
                    pe.wait_ge(x_loaded[layer], line(i, 16, 16 * (c + 1)))
                    transposes(dst, [xin[:, layer, t, :] for t in range(TB)], ready[kind])
                elif kind == "key":
                    if layer == 2:
                        pe.wait_ge(done["x1T"], count("x1T", 1, c))
                        src = x1T[:]
                    else:
                        pe.wait_ge(done["xT"], count("xT"))
                        src = xT[:, layer]
                    nc.tensor.matmul(dst[:], kWT[:, layer], src, start=True, stop=True).then_inc(ready[kind], 1)
                elif kind == "value":
                    if layer == 2:
                        pe.wait_ge(done["yT"], count("yT", 0, c))
                        src = yT
                    else:
                        src = xT[:, layer]
                    w = vWT[:, layer].rearrange("p (g e d) -> p g e d", g=HP, e=2)
                    for b in range(BB):
                        for e in range(2):
                            last = nc.tensor.matmul(dst[e * S:(e + 1) * S, b * S:(b + 1) * S],
                                                    src[:, b * S:(b + 1) * S], w[:, :, e, :], start=True, stop=True)
                    last.then_inc(ready[kind], 1)
                elif kind == "attT":
                    pe.wait_ge(att_done, tile_no(i, layer, c, TB))
                    transposes(dst, [att[:, layer, t, :] for t in range(TB)], ready[kind])
                elif kind == "proj":
                    pe.wait_ge(done["attT"], count("attT"))
                    if layer == 2:
                        pe.wait_ge(padded, line(i, 1, c + 1))
                    nc.tensor.matmul(dst[:], oWT[:, layer], attT[:], start=True, stop=True).then_inc(ready[kind], 1)
                elif kind == "norm1":
                    pe.wait_ge(done["proj"], count("proj"))
                    transposes(dst, [zT[:, t * P:(t + 1) * P] for t in range(TB)], ready[kind])
                elif kind == "x1T":
                    pe.wait_ge(done["norm1"], count("norm1"))
                    transposes(dst, [zn[:, t, :] for t in range(TB)], ready[kind])
                elif kind == "ff1":
                    pe.wait_ge(done["x1T"], count("x1T"))
                    nc.tensor.matmul(dst[:], w1T[:, ffn[layer], chunk * P:(chunk + 1) * P], xfT[:],
                                     start=True, stop=True).then_inc(ready[kind], 1)
                elif kind == "ff2":
                    pe.wait_ge(done["ff1"], job_count(i, "ff1", layer, c, FC - 1))
                    for n in range(FC):
                        last = nc.tensor.matmul(dst[:], w2T[:, ffn[layer], n, :], hT[:, n, :],
                                                start=(n == 0), stop=(n == FC - 1))
                    last.then_inc(ready[kind], 1)
                elif kind == "norm2":
                    pe.wait_ge(done["ff2"], count("ff2"))
                    transposes(dst, [rT[:, t * P:(t + 1) * P] for t in range(TB)], ready[kind])
                elif kind == "yT":
                    pe.wait_ge(done["norm2"], count("norm2"))
                    transposes(dst, [rn[:, t, :] for t in range(TB)], ready[kind])

            def step(i, r):
                for lag, stage in ((-1, scores), (3, weighted), (1, causal)):
                    layer, c, t = at_step(r - lag)
                    if exists(i, c):
                        stage(i, layer, c, t)
                for one in SCHEDULE[r][0]:
                    if exists(i, one[2]):
                        job(i, *one)
                layer, c, t = at_step(r - 2)
                if exists(i, c):
                    logitsT(i, layer, c, t)
                for one in SCHEDULE[r][1]:
                    if exists(i, one[2]):
                        job(i, *one)

            rounds(pe, step)

        @block.scalar
        def _(act):
            eps_log, eps_ln, tiny, one = (small[:, n:n + 1] for n in (2, 1, 0, 3))
            nc.scalar.preload_act_table_set("natural_log_exp_and_others")
            act.wait_ge(setup_pool, 1)
            act.wait_ge(loaded, 48)
            nc.scalar.activation(gam[:, 1, :], gam[:, 0, :], ACT.Abs).then_inc(setup_act, 1)
            nc.scalar.activation(ge.rearrange("p l h s c -> p (l h s c)"), ge.rearrange("p l h s c -> p (l h s c)"),
                                 ACT.Ln, bias=eps_log).then_inc(setup_act, 1)
            act.wait_ge(setup_act, 2)
            nc.scalar.activation(gam[:, 2, :], gam[:, 1, :], ACT.Exp, scale=-1.0).then_inc(setup_act, 1)
            act.wait_ge(setup_act, 3)
            nc.scalar.activation(gam[:, 3, :], gam[:, 2, :], ACT.Ln, bias=one).then_inc(setup_act, 1)
            act.wait_ge(weights_loaded, WEIGHT_LOADS * 16)
            targets = [(cols[:].rearrange("p n l -> p (n l)"), psT[:, 0:8 * L]), (b1c[:].rearrange("p l c -> p (l c)"), psT[:, 8 * L:(8 + FC) * L]),
                       (kWT[:].rearrange("p l d -> p (l d)"), psS[0][:, 0:L * D]), (vWT[:].rearrange("p l d -> p (l d)"), psS[1][:, 0:L * D]),
                       (oWT[:].rearrange("p l d -> p (l d)"), psS[2][:, 0:L * D]), (w1T[:, 0], psS[3][:]), (w1T[:, 1], psS[0][:]),
                       (w2T[:, 0].rearrange("p c d -> p (c d)"), psS[1][:]), (w2T[:, 1].rearrange("p c d -> p (c d)"), psS[2][:])]
            for n, (dst, src) in enumerate(targets):
                act.wait_ge(wT_ready, max(n, 1))
                nc.scalar.copy(dst, src).then_inc(wT_done, 1)
            act.wait_ge(setup_dve, SETUP_DVE)
            act.wait_ge(setup_pool, SETUP_POOL)

            def exp1(i, layer, c, t):
                n = tile_no(i, layer, c, t)
                act.wait_ge(shift1_done, n + 1)
                nc.scalar.activation(E[t][:, 0:H * S], E[t][:, 0:H * S], ACT.Exp).then_inc(exp1_done, 1)

            def decays(i, layer, c, t):
                n = tile_no(i, layer, c, t)
                act.wait_ge(dist_done, n + 1)
                nc.scalar.activation(W[t][:], W[t][:], ACT.Ln, bias=tiny).then_inc(log_done, 1)
                act.wait_ge(log_done, n + 1)
                nc.scalar.activation(W[t][:], W[t][:], ACT.Exp, scale=0.5).then_inc(root_done, 1)
                act.wait_ge(root_done, n + 1)
                nc.scalar.activation(W[t][:], W[t][:], ACT.Exp, scale=-1.0).then_inc(te_done, 1)

            def probs(i, layer, c, t):
                n = tile_no(i, layer, c, t)
                act.wait_ge(logitsT_ready, n + 1)
                after(act, weighted_ready, n + 1 - 2)
                nc.scalar.activation(PT[t % 2][:].rearrange("p g q -> p (g q)"), psT[:], ACT.Exp).then_inc(probs_done, 1)

            def rstd_of(i, kind, layer, c):
                n = norm_no(i, kind, layer, c)
                act.wait_ge(stats_step, n * 9 + 9)
                nc.scalar.activation(lvar[:], var4[:], ACT.Ln, scale=0.25, bias=eps_ln).then_inc(lvar_done, 1)
                act.wait_ge(lvar_done, n + 1)
                nc.scalar.activation(rstd[:], lvar[:], ACT.Exp, scale=-0.5).then_inc(rstd_done, 1)

            def job(i, kind, layer, c, chunk):
                me = (kind, layer, c, chunk)
                src = bank(me)
                mine = job_count(i, kind, layer, c, chunk)
                column = lambda n: cols[:, n, layer:layer + 1]
                if kind in ("norm1", "norm2"):
                    rstd_of(i, kind, layer, c)
                if kind not in ("xT", "key", "value", "attT", "x1T", "ff1", "yT"):
                    return
                act.wait_ge(ready[kind], mine)
                if kind == "xT":
                    after(act, done["proj"], job_count(i, "proj", layer, c - 1) if exists(i, c - 1) else 0)
                    nc.scalar.copy(xT[:, layer], src[:]).then_inc(done[kind], 1)
                elif kind == "key":
                    after(act, scores_ready, tile_no(i, layer, c - 1, TB) if exists(i, c - 1) else 0)
                    nc.scalar.activation(kh[:, layer], src[:], ACT.Identity, scale=0.5, bias=column(HKB)).then_inc(done[kind], 1)
                elif kind == "value":
                    after(act, weighted_ready, tile_no(i, layer, c - 1, TB) if exists(i, c - 1) else 0)
                    for e in range(2):
                        rows = slice(e * S, (e + 1) * S)
                        nc.scalar.copy(vx[layer][rows, :, :, e * DK:(e + 1) * DK],
                                       src[rows].rearrange("p (b g d) -> p b g d", b=BB, g=HP)).then_inc(done[kind], 1)
                elif kind == "attT":
                    after(act, ready["proj"], mine - 1)
                    nc.scalar.activation(attT[:], src[:], ACT.Identity, bias=column(VB)).then_inc(done[kind], 1)
                    if layer == 2:
                        act.wait_ge(done[kind], mine)
                        nc.scalar.copy(attT[:].rearrange("p (b q) -> p b q", b=BB)[:, :, 0:1],
                                       zeros[:, 0:BB].unsqueeze(2)).then_inc(padded, 1)
                elif kind == "x1T":
                    dst = x1T if layer == 1 else xfT
                    if layer == 1 and exists(i, c - 1):
                        act.wait_ge(done["proj"], job_count(i, "proj", 2, c - 1))
                        act.wait_ge(ready["key"], job_count(i, "key", 2, c - 1))
                    if layer != 1:
                        after(act, done["ff2"], ffn_no(i, layer, c))
                    nc.scalar.activation(dst[:], src[:], ACT.Identity, scale=column(G1), bias=column(B1)).then_inc(done[kind], 1)
                elif kind == "ff1":
                    after(act, ready["ff2"], ffn_no(i, layer, c))
                    nc.scalar.activation(hT[:, chunk], src[:], ACT.Relu, bias=b1c[:, layer, chunk:chunk + 1]).then_inc(done[kind], 1)
                elif kind == "yT":
                    if exists(i, c - 1):
                        act.wait_ge(ready["value"], job_count(i, "value", 2, c - 1))
                    nc.scalar.activation(yT[:], src[:], ACT.Identity, scale=column(G2), bias=column(B2)).then_inc(done[kind], 1)

            def step(i, r):
                for lag, stage in ((3, probs), (2, decays)):
                    layer, c, t = at_step(r - lag)
                    if exists(i, c):
                        stage(i, layer, c, t)
                for one_job in SCHEDULE[r][0]:
                    if exists(i, one_job[2]):
                        job(i, *one_job)
                layer, c, t = at_step(r)
                if exists(i, c):
                    exp1(i, layer, c, t)
                for one_job in SCHEDULE[r][1]:
                    if exists(i, one_job[2]):
                        job(i, *one_job)

            rounds(act, step)

        @block.vector
        def _(dve):
            count = [0]

            def setup(ins):
                count[0] += 1
                ins.then_inc(setup_dve, 1)
                dve.wait_ge(setup_dve, count[0])

            dve.wait_ge(setup_act, 2)
            flat = lambda a: a.rearrange("p l h s c -> p (l h s c)")
            setup(nc.vector.tensor_tensor(flat(al), flat(al), flat(ge), ALU.subtract))
            dve.wait_ge(setup_pool, 2)
            setup(nc.vector.tensor_tensor(hidden[:, :, :, S:SKEW].rearrange("p l h s -> p (l h) s"),
                                          al[:, :, :, :, 0].rearrange("p l h s -> p (l h) s"),
                                          al[:, :, :, :, 1].rearrange("p l h s -> p (l h) s"), ALU.is_ge))
            setup(nc.vector.tensor_scalar(hidden[:].rearrange("p l h u -> p (l h u)"),
                                          hidden[:].rearrange("p l h u -> p (l h u)"), NEG, None, ALU.mult))
            dve.wait_ge(setup_act, 4)
            setup(nc.vector.scalar_tensor_tensor(gam[:, 4, :], gam[:, 0, :], 0.0, gam[:, 3, :], ALU.max, ALU.add))
            setup(nc.vector.tensor_tensor(gam[:, 4, :], gam[:, 4, :], gam[:, 4, :], ALU.mult))
            dve.wait_ge(setup_pool, 5)
            for l in range(L):
                setup(nc.vector.tensor_tensor(per_head(decay[:, l]), per_head(dist_ij[:]),
                                              over_keys(gam[:, 4, l * H:(l + 1) * H]), ALU.mult))
            dve.wait_ge(wT_done, 1)
            setup(nc.vector.tensor_scalar(cols[:, HKB, :], cols[:, HKB, :], 0.5, None, ALU.mult))
            dve.wait_ge(wT_done, 9)
            for n in range(L):
                setup(nc.vector.memset(kx[n][:].rearrange("p h t -> p (h t)"), 0.0))
                setup(nc.vector.memset(vx[n][:].rearrange("p b g c -> p (b g c)"), 0.0))
                for e in range(2):
                    setup(nc.vector.memset(vx[n][e * S:(e + 1) * S, :, :, 2 * DK + e:2 * DK + e + 1], 1.0))
            for t in range(TB):
                setup(nc.vector.memset(E[t][:, H * S:H * S + 1], 0.0))
            assert count[0] == SETUP_DVE, count[0]
            dve.wait_ge(setup_pool, SETUP_POOL)

            def shift1(i, layer, c, t):
                n = tile_no(i, layer, c, t)
                dve.wait_ge(scores_ready, n + 1)
                nc.vector.tensor_reduce(neg1[:, t], per_head(psS[t][:]), AX_X, ALU.max, negate=True).then_inc(max1_done, 1)
                dve.wait_ge(max1_done, n + 1)
                after(dve, tree_step, tile_no(i, layer, c, t - TB) * 6 + 1 if isinstance(i, int) else line(i, 3 * TB * 6, 6 * (TB * (3 * c + (4 if layer == 2 else layer - 1)) + t - TB) + 1))
                nc.vector.tensor_tensor(per_head(E[t][:, 0:H * S]), per_head(psS[t][:]), over_keys(neg1[:, t]),
                                        ALU.add).then_inc(shift1_done, 1)

            def scan(i, layer, c, t):
                n = tile_no(i, layer, c, t)
                dve.wait_ge(exp1_done, n + 1)
                after(dve, logitsT_ready, n + 1 - TB)
                nc.vector.tensor_tensor_scan(W[t][:, ::-1], E[t][:, 1:H * S + 1][:, ::-1], keep[:, BMASK[layer]][:, ::-1],
                                             0.0, ALU.add, ALU.mult).then_inc(scan_done, 1)
                dve.wait_ge(tree_step, tile_no(i, layer, c, t + 1) * 6 if isinstance(i, int) else line(i, 3 * TB * 6, 6 * (TB * (3 * c + (4 if layer == 2 else layer - 1)) + t + 1)))
                nc.vector.reciprocal(rden1[:, t], den1[:, t]).then_inc(rden1_done, 1)

            def logits(i, layer, c, t):
                n = tile_no(i, layer, c, t)
                dve.wait_ge(te_done, n + 1)
                dve.wait_ge(causal_ready, n + 1)
                nc.vector.scalar_tensor_tensor(W[t][:], W[t][:], TE_MIN, psS[t][:], ALU.max, ALU.mult).then_inc(logits_done, 1)
                dve.wait_ge(logits_done, n + 1)
                nc.vector.tensor_reduce(neg2[:, t], per_head(W[t][:]), AX_X, ALU.max, negate=True).then_inc(max2_done, 1)
                dve.wait_ge(max2_done, n + 1)
                nc.vector.tensor_tensor(per_head(W[t][:]), per_head(W[t][:]), over_keys(neg2[:, t]), ALU.add).then_inc(shift2_done, 1)

            def attend(i, layer, c, t):
                n = tile_no(i, layer, c, t)
                o = psO[:, 0:HP * VW].rearrange("p (g c) -> p g c", g=HP)
                dve.wait_ge(weighted_ready, n + 1)
                nc.vector.reciprocal(rden2[:, t], o[:, :, 2 * DK:VW]).then_inc(rden2_done, 1)
                dve.wait_ge(rden2_done, n + 1)
                if t == 0:
                    after(dve, ready["attT"], job_count(i, "attT", layer, c - 1) if exists(i, c - 1) else 0)
                nc.vector.tensor_tensor(att[:, layer, t].rearrange("p (g e d) -> p g e d", g=HP, e=2),
                                        o[:, :, 0:2 * DK].rearrange("p g (e d) -> p g e d", e=2),
                                        rden2[:, t].unsqueeze(3).to_broadcast([P, HP, 2, DK]), ALU.mult).then_inc(att_done, 1)

            def normalise(i, kind, layer, c, src, dst, free_sem, free_count):
                n = norm_no(i, kind, layer, c)
                after(dve, rstd_done, n)
                dve.wait_ge(ready[kind], job_count(i, kind, layer, c))
                for t in range(TB):
                    nc.vector.bn_stats(stats[:, t], src[:, t * D:(t + 1) * D]).then_inc(stats_step, 1)
                even, odd = stats[:, :, 1:3], stats[:, :, 4:6]
                dve.wait_ge(stats_step, n * 9 + 4)
                nc.vector.tensor_tensor(mv[:, :, 0:2], even, odd, ALU.add).then_inc(stats_step, 1)
                nc.vector.tensor_tensor(mv[:, :, 2], stats[:, :, 1], stats[:, :, 4], ALU.subtract).then_inc(stats_step, 1)
                dve.wait_ge(stats_step, n * 9 + 6)
                nc.vector.tensor_tensor(mv[:, :, 3], mv[:, :, 2], mv[:, :, 2], ALU.mult).then_inc(stats_step, 1)
                nc.vector.tensor_scalar(mean[:], mv[:, :, 0], 0.5, None, ALU.mult).then_inc(stats_step, 1)
                dve.wait_ge(stats_step, n * 9 + 8)
                nc.vector.scalar_tensor_tensor(var4[:], mv[:, :, 1], 4.0 / D, mv[:, :, 3], ALU.mult, ALU.add).then_inc(stats_step, 1)
                dve.wait_ge(rstd_done, n + 1)
                after(dve, free_sem, free_count)
                for t in range(TB):
                    last = nc.vector.tensor_scalar(dst[:, t], src[:, t * D:(t + 1) * D], mean[:, t:t + 1], rstd[:, t:t + 1],
                                                   ALU.subtract, ALU.mult)
                last.then_inc(done[kind], 1)

            def job(i, kind, layer, c, chunk):
                src = bank((kind, layer, c, chunk))
                mine = job_count(i, kind, layer, c, chunk)
                column = lambda n: cols[:, n, layer:layer + 1]
                if kind == "proj":
                    dve.wait_ge(ready[kind], mine)
                    after(dve, ready["norm1"], mine - 1)
                    residual = x1T[:] if layer == 2 else xT[:, layer]
                    nc.vector.scalar_tensor_tensor(zT[:], src[:], column(OB), residual, ALU.add, ALU.add).then_inc(done[kind], 1)
                elif kind == "ff2":
                    dve.wait_ge(ready[kind], mine)
                    after(dve, ready["norm2"], mine - 1)
                    nc.vector.scalar_tensor_tensor(rT[:], src[:], column(BF2), xfT[:], ALU.add, ALU.add).then_inc(done[kind], 1)
                elif kind == "norm1":
                    normalise(i, kind, layer, c, src, zn, ready["x1T"], mine - 1)
                elif kind == "norm2":
                    if layer == 2:
                        normalise(i, kind, layer, c, src, rn, ready["yT"], min(i + c + 2, GROUPS) if isinstance(i, int) else line(i, 1, c + 2))
                    else:
                        normalise(i, kind, layer, c, src, rn, out_scaled, max(i + c - 1, 0) if isinstance(i, int) else line(i, 1, c - 1))

            def step(i, r):
                for lag, stage in ((0, shift1), (4, attend)):
                    layer, c, t = at_step(r - lag)
                    if exists(i, c):
                        stage(i, layer, c, t)
                for one in SCHEDULE[r][0]:
                    if exists(i, one[2]):
                        job(i, *one)
                for lag, stage in ((1, scan), (2, logits)):
                    layer, c, t = at_step(r - lag)
                    if exists(i, c):
                        stage(i, layer, c, t)
                for one in SCHEDULE[r][1]:
                    if exists(i, one[2]):
                        job(i, *one)

            rounds(dve, step)

        @block.gpsimd
        def _(pool):
            count = [0]

            def setup(ins):
                count[0] += 1
                ins.then_inc(setup_pool, 1)
                pool.wait_ge(setup_pool, count[0])

            for n, value in enumerate((TINY, EPS_LN, EPS_LOG, 1.0)):
                last = nc.gpsimd.memset(small[:, n:n + 1], value)
            setup(last)
            setup(nc.gpsimd.memset(hidden[:, :, :, 0:S], 0.0))
            setup(nc.gpsimd.memset(identf[:], 0.0))
            setup(nc.gpsimd.affine_select(out=identf[:], in_=identf[:], compare_op=ALU.not_equal, fill=1.0, base=0,
                                          pattern=[[-1, P]], channel_multiplier=1))
            for n in range(BT):
                last = nc.gpsimd.iota(per_head(dist_ij[n * S:(n + 1) * S]), pattern=[[0, H], [-1, S]], base=0,
                                      channel_multiplier=1, allow_small_or_imprecise_dtypes=True)
            setup(last)
            setup(nc.gpsimd.memset(identb[:], 0.0))
            setup(nc.gpsimd.affine_select(out=identb[:], in_=identb[:], compare_op=ALU.not_equal, fill=1.0, base=0,
                                          pattern=[[-1, P]], channel_multiplier=1))
            setup(nc.gpsimd.memset(zeros[:], 0.0))
            for m in range(2):
                for n in range(BT):
                    rows = slice(n * S, (n + 1) * S)
                    setup(nc.gpsimd.affine_select(out=per_head(causal_bias[rows, m]), in_=per_head(zeros[rows]), compare_op=ALU.is_gt,
                                                  fill=NEG, base=m, pattern=[[0, H], [-1, S]], channel_multiplier=1))
                    setup(nc.gpsimd.affine_select(out=per_head(keep[rows, m]), in_=per_head(zeros[rows]), compare_op=ALU.is_ge,
                                                  fill=1.0, base=1 - m, pattern=[[0, H], [1, S]], channel_multiplier=-1))
            for m in range(2):
                setup(nc.gpsimd.memset(per_head(keep[:, m])[:, :, S - 1:S], 0.0))
            pool.wait_ge(skew_read, 16 * BT)
            for l in range(L):
                for n in range(BT):
                    rows = slice(n * S, (n + 1) * S)
                    setup(nc.gpsimd.affine_select(out=per_head(mask_bias[rows, l]), in_=shifted_mask[rows, l], compare_op=ALU.is_ge,
                                                  fill=0.0, base=-BMASK[l], pattern=[[0, H], [1, S]], channel_multiplier=-1))
            assert count[0] == SETUP_POOL, count[0]

            def six(i, layer, c, t, k):
                if isinstance(i, int):
                    return 6 * tile_no(i, layer, c, t) + k
                return line(i, 3 * TB * 6, 6 * (TB * (3 * c + (4 if layer == 2 else layer - 1)) + t) + k)

            def sums(i, layer, c, t):
                pool.wait_ge(exp1_done, tile_no(i, layer, c, t) + 1)
                src = per_head(E[t][:, 0:H * S])
                for k, half in enumerate((32, 16, 8, 4, 2, 1)):
                    after(pool, tree_step, six(i, layer, c, t, k))
                    dst = tree[k][:] if half > 1 else den1[:, t].unsqueeze(2)
                    nc.gpsimd.tensor_tensor(dst, src[:, :, 0:half], src[:, :, half:2 * half], ALU.add).then_inc(tree_step, 1)
                    src = dst

            def distances(i, layer, c, t):
                n = tile_no(i, layer, c, t)
                pool.wait_ge(scan_done, n + 1)
                nc.gpsimd.tensor_tensor(W[t][:], W[t][:], decay[:, layer], ALU.mult).then_inc(decay_done, 1)
                pool.wait_ge(decay_done, n + 1)
                pool.wait_ge(rden1_done, n + 1)
                nc.gpsimd.tensor_tensor(per_head(W[t][:]), per_head(W[t][:]), over_keys(rden1[:, t]), ALU.mult).then_inc(dist_done, 1)

            def job(i, kind, layer, c, chunk):
                if kind == "norm2" and layer == 2:
                    pool.wait_ge(done["norm2"], job_count(i, "norm2", layer, c))
                    wide = lambda a: a[:].unsqueeze(1).to_broadcast([P, TB, D])
                    after(pool, stored, line(i, 16, 16 * c))
                    nc.gpsimd.tensor_tensor(outb[:], rn[:], wide(g2row), ALU.mult).then_inc(out_scaled, 1)
                    pool.wait_ge(out_scaled, line(i, 1, c + 1))
                    nc.gpsimd.tensor_tensor(outb[:], outb[:], wide(b2row), ALU.add).then_inc(out_done, 1)

            def step(i, r):
                layer, c, t = at_step(r - 1)
                if exists(i, c):
                    sums(i, layer, c, t)
                for one in SCHEDULE[r][0]:
                    if exists(i, one[2]):
                        job(i, *one)
                if exists(i, c):
                    distances(i, layer, c, t)
                for one in SCHEDULE[r][1]:
                    if exists(i, one[2]):
                        job(i, *one)

            rounds(pool, step)


WEIGHT_LOADS = 3 + 4 + 8 + 1 + 2
SETUP_DVE = 9 + 4 * L + TB
SETUP_POOL = 8 + 8 + 2 + 2 * L


_INS = ["x", "ctx_1024", "L0_xattn_kW", "L0_xattn_kb", "L0_xattn_vW", "L0_xattn_vb", "L0_xattn_oW", "L0_xattn_ob",
        "L0_xattn_gammas", "L0_xattn_alphas", "L0_xattn_ln1_g", "L0_xattn_ln1_b", "L0_xattn_w1", "L0_xattn_b1",
        "L0_xattn_w2", "L0_xattn_b2", "L0_xattn_ln2_g", "L0_xattn_ln2_b", "L0_xattn_gumbel_E"]


def kernel(**inputs):
    import numpy as _np
    import concourse.bacc as _bacc
    from concourse import mybir as _mybir
    from concourse.bass_utils import run_bass_kernel_spmd as _run

    nc = _bacc.Bacc("TRN2", target_bir_lowering=False, num_devices=1)
    arrays, args = {}, []
    for name in _INS:
        a = _np.ascontiguousarray(inputs[name])
        arrays[f"in_{name}"] = a
        args.append(nc.dram_tensor(f"in_{name}", a.shape, _mybir.dt.from_np(a.dtype), kind="ExternalInput").ap())
    out = nc.dram_tensor("out_0", (B, S, D), F32, kind="ExternalOutput").ap()
    build(nc, *args, out)
    r = _run(nc, [arrays], core_ids=[0])
    return r.results[0]["out_0"]
```

```python
from contextlib import ExitStack

import concourse.bass as bass
from concourse import mybir

ALU = mybir.AluOpType
ACT = mybir.ActivationFunctionType
AX_X = mybir.AxisListType.X
F32 = mybir.dt.float32
BF16 = mybir.dt.bfloat16

P = 128
B, S, D, H, DFF, L = 128, 64, 128, 8, 512, 3
DK = D // H
BT = P // S
TB = 4
GROUPS = B // (BT * TB)
TOK = TB * P
BB = BT * TB
HP = H // 2
VW = 2 * DK + 2
FC = DFF // P
STEPS = L * TB
NEG = -1e32
TINY = 1e-30
EPS_LN = 1e-5
EPS_LOG = 1e-5
TE_MIN = 1e-5
BMASK = (1, 1, 0)
SKEW = 2 * S

PARTS = 3
SCHEDULE = {
    0: [("attT", 1, -1, 0), ("ff2", 0, -1, 0)], 2: [("proj", 1, -1, 0), ("mean", 0, -1, 2)],
    3: [("xT", 1, 0, 0)], 4: [("var", 0, -1, 2)], 5: [("key", 1, 0, 0)],
    6: [("value", 0, 0, 0)], 8: [("value", 1, 0, 0)], 9: [("mean", 1, -1, 1)],
    10: [("attT", 2, -2, 0)], 11: [("var", 1, -1, 1)], 12: [("proj", 2, -2, 0)],
    14: [("mean", 2, -2, 1)], 15: [("key", 2, -1, 0)], 16: [("var", 2, -2, 1)], 17: [("value", 2, -1, 0)],
    20: [("ff1", 2, -2, 0), ("ff1", 2, -2, 1)], 21: [("ff1", 2, -2, 2), ("ff1", 2, -2, 3)],
    22: [("attT", 0, 0, 0)], 23: [("ff2", 2, -2, 0)], 24: [("proj", 0, 0, 0)], 25: [("mean", 2, -2, 2)],
    26: [("xT", 0, 1, 0)], 27: [("mean", 0, 0, 1), ("var", 2, -2, 2)], 28: [("key", 0, 1, 0)],
    29: [("var", 0, 0, 1)], 31: [("out", 2, -2, 0)],
    33: [("ff1", 0, 0, 0), ("ff1", 0, 0, 1)], 34: [("ff1", 0, 0, 2), ("ff1", 0, 0, 3)],
}
ORDER = [job for part in sorted(SCHEDULE) for job in SCHEDULE[part]]
JOB_BANKS = 4


def spread_banks():
    left, banks = [0] * JOB_BANKS, []
    for part in sorted(SCHEDULE):
        for job in SCHEDULE[part]:
            banks.append(min(range(JOB_BANKS), key=lambda n: left[n]))
            left[banks[-1]] = part + (4.5 if job[0] == "mean" else 1.5) + 0.01 * len(banks)
    return banks


BANK = spread_banks()
FIRST_ROUND, LOOP_FROM, LOOP_TO, LAST_ROUND = -1, 2, GROUPS - 2, GROUPS + 1


def exists(i, c):
    return not isinstance(i, int) or 0 <= i + c < GROUPS


def line(i, a, b):
    return i * a + b


def block_no(i, layer, c):
    if isinstance(i, int):
        k = i + c
        return 2 * min(k + 2, GROUPS) + k if layer == 2 else 2 * k + max(k - 1, 0) + layer
    return line(i, 3, 3 * c + (4 if layer == 2 else layer - 1))


def tile_no(i, layer, c, t):
    if isinstance(i, int):
        return TB * block_no(i, layer, c) + t
    return line(i, 3 * TB, TB * (3 * c + (4 if layer == 2 else layer - 1)) + t)


def ffn_no(i, layer, c):
    if isinstance(i, int):
        k = i + c
        return min(k + 2, GROUPS) + k if layer == 2 else k + max(k - 1, 0)
    return line(i, 2, 2 * c + (2 if layer == 2 else -1))


def norm_no(i, layer, c, which):
    norms = [(n, job) for n, job in enumerate(ORDER) if job[0] == "mean"]
    place, own = next((n, job[2]) for n, job in norms if job[1] == layer and job[3] == which)
    i, past = i + (c - own), LOOP_FROM

    def before(last):
        return sum(exists(n, job[2]) and (n < last or j < place)
                   for n in range(FIRST_ROUND, last + 1) for j, job in norms)

    return before(i) if isinstance(i, int) else line(i, len(norms), before(past) - past * len(norms))


def job_count(i, kind, layer, c, chunk=0):
    if kind == "ff1":
        if isinstance(i, int):
            return FC * ffn_no(i, layer, c) + chunk + 1
        return line(i, 2 * FC, FC * (2 * c + (2 if layer == 2 else -1)) + chunk + 1)
    if kind == "ff2":
        return ffn_no(i, layer, c) + 1
    if kind == "xT":
        return line(i, 2, 2 * c + layer + 1)
    if kind == "out":
        return line(i, 1, c + 1)
    if kind in ("mean", "var"):
        return norm_no(i, layer, c, chunk) + 1
    return block_no(i, layer, c) + 1


def after(eng, sem, count):
    if not isinstance(count, int) or count > 0:
        eng.wait_ge(sem, count)


def jobs_in(part, late=0):
    past, part = divmod(part - late, PARTS * STEPS)
    return [(ORDER.index(j), j[0], j[1], j[2] + past, j[3]) for j in SCHEDULE.get(part, [])]


def at_step(r):
    d, r = divmod(r, STEPS)
    layer = r // TB
    return layer, d - (layer == 2), r % TB


def rounds(eng, step):
    for i in range(FIRST_ROUND, LOOP_FROM):
        for r in range(STEPS):
            step(i, r)
    with eng.Fori(LOOP_FROM, LOOP_TO) as i:
        for r in range(STEPS):
            step(i, r)
    for i in range(LOOP_TO, LAST_ROUND + 1):
        for r in range(STEPS):
            step(i, r)


def build(nc, x, ctx, kW, kb, vW, vb, oW, ob, gammas, alphas, ln1_g, ln1_b, w1, b1, w2, b2, ln2_g, ln2_b,
          gumbel, out):
    with ExitStack() as stack:
        def sb(name, shape, dt=F32):
            return stack.enter_context(nc.sbuf_tensor(name, shape, dt))

        def sem(name):
            return stack.enter_context(nc.semaphore(name))

        psS = [stack.enter_context(nc.psum_tensor(f"psS{n}", [P, TOK], F32)) for n in range(2)]
        psT = stack.enter_context(nc.psum_tensor("psT", [P, TOK], F32))
        psO = stack.enter_context(nc.psum_tensor("psO", [P, TOK], F32))
        psJ = [stack.enter_context(nc.psum_tensor(f"psJ{n}", [P, TOK], F32)) for n in range(JOB_BANKS)]

        identf = sb("identf", [P, P])
        identb = sb("identb", [P, P], BF16)
        mask_bias = sb("mask_bias", [P, L, H * S], BF16)
        causal_bias = sb("causal_bias", [P, 2, H * S], BF16)
        keep = sb("keep", [P, 2, H * S])
        decay = sb("decay", [P, L, H * S])
        kWT = sb("kWT", [P, L, D])
        vWT = sb("vWT", [P, L, D])
        oWT = sb("oWT", [P, L, D])
        w1T = sb("w1T", [P, 2, DFF])
        w2T = sb("w2T", [P, 2, FC, D])
        cols = sb("cols", [P, 8, L])
        HKB, VB, OB, G1, B1, BF2, G2, B2 = range(8)
        b1c = sb("b1c", [P, L, FC])
        vectors = sb("vectors", [(8 + FC) * L, D])
        small = sb("small", [P, 4])
        xin = sb("xin", [P, 2, TB, D])
        xT = sb("xT", [P, 2, TOK])
        x1T = sb("x1T", [P, TOK])
        xfT = sb("xfT", [P, TOK])
        yT = sb("yT", [P, TOK])
        kh = sb("kh", [P, L, TOK])
        kx = [sb(f"kx{n}", [P, H, TOK]) for n in range(L)]
        vx = [sb(f"vx{n}", [P, BB, HP, VW]) for n in range(L)]
        E = [sb(f"E{n}", [P, H * S + 1]) for n in range(TB)]
        W = [sb(f"W{n}", [P, H * S]) for n in range(TB)]
        raw = [sb(f"raw{n}", [P, H * S]) for n in range(TB)]
        PT = [sb(f"PT{n}", [P, HP, P]) for n in range(2)]
        tree = [sb(f"tree{n}", [P, H, n]) for n in (32, 16, 8)]
        neg1 = sb("neg1", [P, TB, H])
        den1 = sb("den1", [P, TB, H])
        rden1 = sb("rden1", [P, TB, H])
        neg2 = sb("neg2", [P, TB, H])
        rden2 = sb("rden2", [P, TB, HP, 2])
        att = sb("att", [P, L, TB, D])
        attT = sb("attT", [P, TOK])
        zT = sb("zT", [P, TOK])
        square = sb("square", [P, TOK])
        rstd = sb("rstd", [P, TOK])
        normed = sb("normed", [P, TOK])
        outT = sb("outT", [P, TOK])
        centre = sb("centre", [P, P])
        average = sb("average", [P, P])
        hT = sb("hT", [P, FC, TOK])
        rT = sb("rT", [P, TOK])
        outb = sb("outb", [P, TB, D])
        flat0, flat1, flat2 = (k[:].rearrange("p h t -> p (h t)") for k in kx)
        n_nat, n_w = 3 * L * D, 2 * DFF
        natural = flat0[:, 0:n_nat].rearrange("p (n l d) -> p n l d", n=3, l=L)
        w1n = flat0[:, n_nat:n_nat + n_w].rearrange("p (n c d) -> p n c d", n=2, c=FC)
        w2n = flat0[:, n_nat + n_w:n_nat + 2 * n_w].rearrange("p (n f) -> p n f", n=2)
        al = flat1[:, 0:L * H * S * 2].rearrange("p (l h s c) -> p l h s c", l=L, h=H, c=2)
        ge = flat2[:, 0:L * H * S * 2].rearrange("p (l h s c) -> p l h s c", l=L, h=H, c=2)
        hidden = sb("hidden", [P, L, H, SKEW])
        shifted_mask = hT[:].rearrange("p c t -> p (c t)")[:, 0:L * H * S].rearrange("p (l h s) -> p l h s", l=L, h=H)
        gam = sb("gam", [P, 5, L * H])
        zeros = sb("zeros", [P, H * S])
        dist_ij = sb("dist_ij", [P, H * S])
        skew = nc.dram_tensor("skew", [L * H, S * (SKEW + 1)], F32, kind="Internal").ap()

        loaded = sem("loaded")
        weights_loaded = sem("weights_loaded")
        setup_pool = sem("setup_pool")
        setup_act = sem("setup_act")
        setup_dve = sem("setup_dve")
        skew_written = sem("skew_written")
        skew_read = sem("skew_read")
        wT_ready = sem("wT_ready")
        wT_done = sem("wT_done")
        scores_ready = sem("scores_ready")
        max1_done = sem("max1_done")
        shift1_done = sem("shift1_done")
        exp1_done = sem("exp1_done")
        causal_ready = sem("causal_ready")
        raw_done = sem("raw_done")
        tree_step = sem("tree_step")
        den1_done = sem("den1_done")
        rden1_done = sem("rden1_done")
        scan_done = sem("scan_done")
        decay_done = sem("decay_done")
        dist_done = sem("dist_done")
        log_done = sem("log_done")
        root_done = sem("root_done")
        te_done = sem("te_done")
        logits_done = sem("logits_done")
        max2_done = sem("max2_done")
        shift2_done = sem("shift2_done")
        logitsT_ready = sem("logitsT_ready")
        probs_done = sem("probs_done")
        weighted_ready = sem("weighted_ready")
        rden2_done = sem("rden2_done")
        att_done = sem("att_done")
        kinds = ("xT", "key", "value", "attT", "proj", "mean", "var", "ff1", "ff2", "out")
        ready = {k: sem(f"{k}_ready") for k in kinds}
        done = {k: sem(f"{k}_done") for k in kinds}
        x_loaded = [sem(f"x_loaded{n}") for n in range(2)]
        kx_filled = [sem(f"kx_filled{n}") for n in range(L)]
        padded = sem("padded")
        square_done = sem("square_done")
        rstd_done = sem("rstd_done")
        affine_done = sem("affine_done")
        stored = sem("stored")

        x_groups = [a.rearrange("(s t b) q d -> s (b q) t d", t=TB, b=BT) for a in (ctx, x)]
        out_groups = out.rearrange("(s t b) q d -> s (b q) t d", t=TB, b=BT)

        def per_head(ap):
            return ap.rearrange("p (h k) -> p h k", h=H)

        def over_keys(ap):
            return ap.unsqueeze(2).to_broadcast([P, H, S])

        def bank_free(eng, i, place):
            n, back = place, 0
            while not isinstance(i, int) or i + back >= FIRST_ROUND:
                n -= 1
                if n < 0:
                    n, back = len(ORDER) - 1, back - 1
                kind, layer, c, chunk = ORDER[n]
                if BANK[n] == BANK[place] and exists(i, c + back):
                    reads = 2 if kind == "value" else 1
                    after(eng, done[kind], job_count(i, kind, layer, c + back, chunk) * reads)
                    return

        ffn = {0: 0, 2: 1}

        block = stack.enter_context(nc.Block())

        @block.sync
        def _(sp):
            sp.dma_start(al.rearrange("p l h s c -> p (l h s c)"),
                         alphas.rearrange("l h s c -> (l h s c)").partition_broadcast(P)).then_inc(loaded, 16)
            sp.dma_start(ge.rearrange("p l h s c -> p (l h s c)"),
                         gumbel.rearrange("l h s c -> (l h s c)").partition_broadcast(P)).then_inc(loaded, 16)
            sp.dma_start(gam[:, 0, :], gammas.rearrange("l h a b -> (l h a b)").partition_broadcast(P)).then_inc(loaded, 16)
            for n, a in enumerate((kW, vW, oW)):
                sp.dma_start(natural[:, n], a.rearrange("l o i -> o l i")).then_inc(weights_loaded, 16)
            for n, l in enumerate((0, 2)):
                sp.dma_start(w1n[:, n], w1[l].rearrange("(c p) i -> p c i", p=P)).then_inc(weights_loaded, 16)
                sp.dma_start(w2n[:, n], w2[l]).then_inc(weights_loaded, 16)
            for n, a in enumerate((kb, vb, ob, ln1_g, ln1_b, b2, ln2_g, ln2_b)):
                sp.dma_start(vectors[n * L:(n + 1) * L, :], a).then_inc(weights_loaded, 16)
            sp.dma_start(vectors[8 * L:, :], b1.rearrange("l (c p) -> (l c) p", p=P)).then_inc(weights_loaded, 16)
            sp.wait_ge(setup_dve, 3)
            sp.dma_start(bass.AP(skew.tensor, 0, [[SKEW + 1, S], [S * (SKEW + 1), L * H], [1, SKEW]]),
                         hidden[0:S].rearrange("p l h u -> p (l h) u")).then_inc(skew_written, 16)
            sp.wait_ge(skew_written, 16)
            for n in range(BT):
                sp.dma_start(shifted_mask[n * S:(n + 1) * S].rearrange("p l h k -> p (l h) k"),
                             bass.AP(skew.tensor, S, [[SKEW, S], [S * (SKEW + 1), L * H], [1, S]])).then_inc(skew_read, 16)

            def step(i, r):
                for part in range(PARTS * r, PARTS * r + PARTS):
                    for _, kind, layer, c, _ in jobs_in(part, 1):
                        if kind == "xT" and exists(i, c) and exists(i, c + 1):
                            sp.wait_ge(ready["xT"], job_count(i, "xT", layer, c))
                            sp.dma_start(xin[:, layer], x_groups[layer][i + (c + 1)]).then_inc(x_loaded[layer], 16)
                        if kind == "key" and exists(i, c):
                            sp.wait_ge(done["key"], job_count(i, "key", layer, c))
                            for h in range(H):
                                rows = slice(h * DK, (h + 1) * DK)
                                sp.dma_start(kx[layer][rows, h, :], kh[rows, layer, :]).then_inc(kx_filled[layer], 16)
                    for _, kind, layer, c, _ in jobs_in(part, 2):
                        if kind == "out" and exists(i, c):
                            sp.wait_ge(done["out"], line(i, 1, c + 1))
                            sp.dma_start(out_groups[i + c], outb[:]).then_inc(stored, 16)

            for layer in range(2):
                sp.dma_start(xin[:, layer], x_groups[layer][0]).then_inc(x_loaded[layer], 16)
            rounds(sp, step)
            sp.wait_ge(stored, 16 * GROUPS)

        @block.tensor
        def _(pe):
            def transposes(dst, parts, sem_):
                for n, src in enumerate(parts):
                    last = nc.tensor.transpose(dst[:, n * P:(n + 1) * P], src, identf[:])
                last.then_inc(sem_, 1)

            pe.wait_ge(setup_pool, 4)
            pe.wait_ge(weights_loaded, WEIGHT_LOADS * 16)
            rows = (8 + FC) * L
            nc.tensor.transpose(psT[:, 0:rows], vectors[:], identf[0:rows, 0:rows]).then_inc(wT_ready, 1)
            for n in range(3):
                transposes(psJ[n], [natural[:, n, l, :] for l in range(L)], wT_ready)
            for n in range(2):
                if n:
                    pe.wait_ge(wT_done, 3)
                transposes(psJ[3] if not n else psJ[0], [w1n[:, n, c, :] for c in range(FC)], wT_ready)
            for n in range(2):
                pe.wait_ge(wT_done, n + 4)
                transposes(psJ[n + 1], [w2n[:, n, c * P:(c + 1) * P] for c in range(FC)], wT_ready)
            pe.wait_ge(wT_done, 9)
            pe.wait_ge(setup_dve, SETUP_DVE)
            pe.wait_ge(setup_pool, SETUP_POOL)

            def scores(i, layer, c, t):
                n = tile_no(i, layer, c, t)
                after(pe, raw_done, n + 1 - 2)
                if t == 0:
                    pe.wait_ge(done["key"], job_count(i, "key", layer, c))
                    pe.wait_ge(kx_filled[layer], line(i, 16 * H, 16 * H * (c + 1)))
                nc.tensor.matmul(psS[t % 2][:], identb[:], mask_bias[:, layer], start=True, stop=False, skip_group_check=True)
                for b in range(BT):
                    tok = slice((t * BT + b) * S, (t * BT + b + 1) * S)
                    last = nc.tensor.matmul(psS[t % 2][b * S:(b + 1) * S, :], kh[:, layer, tok], kx[layer][:, :, tok],
                                            start=False, stop=True, skip_group_check=True)
                last.then_inc(scores_ready, 1)

            def causal(i, layer, c, t):
                n = tile_no(i, layer, c, t)
                pe.wait_ge(shift1_done, n + 1)
                nc.tensor.matmul(psS[t % 2][:], identb[:], causal_bias[:, BMASK[layer]], start=False, stop=True,
                                 skip_group_check=True).then_inc(causal_ready, 1)

            def logitsT(i, layer, c, t):
                n = tile_no(i, layer, c, t)
                after(pe, probs_done, n)
                pe.wait_ge(shift2_done, n + 1)
                transposes(psT, [W[t][:, g * P:(g + 1) * P] for g in range(HP)], logitsT_ready)

            def weighted(i, layer, c, t):
                n = tile_no(i, layer, c, t)
                after(pe, att_done, n)
                if t == 0:
                    pe.wait_ge(done["value"], job_count(i, "value", layer, c) * 2)
                pe.wait_ge(probs_done, n + 1)
                for b in range(BT):
                    for g in range(HP):
                        last = nc.tensor.matmul(psO[b * S:(b + 1) * S, g * VW:(g + 1) * VW],
                                                PT[t % 2][:, g, b * S:(b + 1) * S], vx[layer][:, t * BT + b, g, :],
                                                start=True, stop=True)
                last.then_inc(weighted_ready, 1)

            def job(i, place, kind, layer, c, chunk):
                dst = psJ[BANK[place]]
                bank_free(pe, i, place)
                count = lambda k, l=layer, cc=c: job_count(i, k, l, cc)
                if kind == "xT":
                    pe.wait_ge(x_loaded[layer], line(i, 16, 16 * (c + 1)))
                    transposes(dst, [xin[:, layer, t, :] for t in range(TB)], ready[kind])
                elif kind == "key":
                    if layer == 2:
                        pe.wait_ge(affine_done, norm_no(i, 1, c, 1) + 1)
                        src = x1T[:]
                    else:
                        pe.wait_ge(done["xT"], count("xT"))
                        src = xT[:, layer]
                    nc.tensor.matmul(dst[:], kWT[:, layer], src, start=True, stop=True).then_inc(ready[kind], 1)
                elif kind == "value":
                    if layer == 2:
                        pe.wait_ge(affine_done, norm_no(i, 0, c, 2) + 1)
                        src = yT
                    else:
                        src = xT[:, layer]
                    w = vWT[:, layer].rearrange("p (g e d) -> p g e d", g=HP, e=2)
                    for b in range(BB):
                        for e in range(2):
                            last = nc.tensor.matmul(dst[e * S:(e + 1) * S, b * S:(b + 1) * S],
                                                    src[:, b * S:(b + 1) * S], w[:, :, e, :], start=True, stop=True)
                    last.then_inc(ready[kind], 1)
                elif kind == "attT":
                    pe.wait_ge(att_done, tile_no(i, layer, c, TB))
                    transposes(dst, [att[:, layer, t, :] for t in range(TB)], ready[kind])
                elif kind == "proj":
                    pe.wait_ge(done["attT"], count("attT"))
                    if layer == 2:
                        pe.wait_ge(padded, line(i, 1, c + 1))
                    nc.tensor.matmul(dst[:], oWT[:, layer], attT[:], start=True, stop=True).then_inc(ready[kind], 1)
                elif kind == "mean":
                    if chunk == 1:
                        pe.wait_ge(done["proj"], count("proj"))
                        src = zT
                    else:
                        pe.wait_ge(done["ff2"], count("ff2"))
                        src = rT
                    nc.tensor.matmul(dst[:], centre[:], src[:], start=True, stop=True).then_inc(ready[kind], 1)
                elif kind == "var":
                    pe.wait_ge(square_done, job_count(i, kind, layer, c, chunk))
                    nc.tensor.matmul(dst[:], average[:], square[:], start=True, stop=True).then_inc(ready[kind], 1)
                elif kind == "ff1":
                    pe.wait_ge(affine_done, norm_no(i, layer, c, 1) + 1)
                    nc.tensor.matmul(dst[:], w1T[:, ffn[layer], chunk * P:(chunk + 1) * P], xfT[:],
                                     start=True, stop=True).then_inc(ready[kind], 1)
                elif kind == "ff2":
                    pe.wait_ge(done["ff1"], job_count(i, "ff1", layer, c, FC - 1))
                    for n in range(FC):
                        last = nc.tensor.matmul(dst[:], w2T[:, ffn[layer], n, :], hT[:, n, :],
                                                start=(n == 0), stop=(n == FC - 1))
                    last.then_inc(ready[kind], 1)
                elif kind == "out":
                    pe.wait_ge(affine_done, norm_no(i, layer, c, 2) + 1)
                    transposes(dst, [outT[:, t * P:(t + 1) * P] for t in range(TB)], ready[kind])

            def stage(i, r, lag, work):
                layer, c, t = at_step(r - lag)
                if exists(i, c):
                    work(i, layer, c, t)

            def jobs(i, part):
                for one in jobs_in(part):
                    if exists(i, one[3]):
                        job(i, *one)

            def step(i, r):
                stage(i, r, 3, logitsT)
                jobs(i, PARTS * r)
                stage(i, r, 0, causal)
                stage(i, r, -1, scores)
                jobs(i, PARTS * r + 1)
                stage(i, r, 3, weighted)
                jobs(i, PARTS * r + 2)

            rounds(pe, step)

        @block.scalar
        def _(act):
            eps_log, eps_ln, tiny, one = (small[:, n:n + 1] for n in (2, 1, 0, 3))
            nc.scalar.preload_act_table_set("natural_log_exp_and_others")
            act.wait_ge(setup_pool, 1)
            act.wait_ge(loaded, 48)
            nc.scalar.activation(gam[:, 1, :], gam[:, 0, :], ACT.Abs).then_inc(setup_act, 1)
            nc.scalar.activation(ge.rearrange("p l h s c -> p (l h s c)"), ge.rearrange("p l h s c -> p (l h s c)"),
                                 ACT.Ln, bias=eps_log).then_inc(setup_act, 1)
            act.wait_ge(setup_act, 2)
            nc.scalar.activation(gam[:, 2, :], gam[:, 1, :], ACT.Exp, scale=-1.0).then_inc(setup_act, 1)
            act.wait_ge(setup_act, 3)
            nc.scalar.activation(gam[:, 3, :], gam[:, 2, :], ACT.Ln, bias=one).then_inc(setup_act, 1)
            act.wait_ge(weights_loaded, WEIGHT_LOADS * 16)
            targets = [(cols[:].rearrange("p n l -> p (n l)"), psT[:, 0:8 * L]), (b1c[:].rearrange("p l c -> p (l c)"), psT[:, 8 * L:(8 + FC) * L]),
                       (kWT[:].rearrange("p l d -> p (l d)"), psJ[0][:, 0:L * D]), (vWT[:].rearrange("p l d -> p (l d)"), psJ[1][:, 0:L * D]),
                       (oWT[:].rearrange("p l d -> p (l d)"), psJ[2][:, 0:L * D]), (w1T[:, 0], psJ[3][:]), (w1T[:, 1], psJ[0][:]),
                       (w2T[:, 0].rearrange("p c d -> p (c d)"), psJ[1][:]), (w2T[:, 1].rearrange("p c d -> p (c d)"), psJ[2][:])]
            for n, (dst, src) in enumerate(targets):
                act.wait_ge(wT_ready, max(n, 1))
                nc.scalar.copy(dst, src).then_inc(wT_done, 1)
            act.wait_ge(setup_dve, SETUP_DVE)
            act.wait_ge(setup_pool, SETUP_POOL)

            def exp1(i, layer, c, t):
                n = tile_no(i, layer, c, t)
                act.wait_ge(shift1_done, n + 1)
                nc.scalar.activation(E[t][:, 0:H * S], E[t][:, 0:H * S], ACT.Exp).then_inc(exp1_done, 1)

            def keep_raw(i, layer, c, t):
                n = tile_no(i, layer, c, t)
                act.wait_ge(causal_ready, n + 1)
                after(act, logits_done, n + 1 - TB)
                nc.scalar.copy(raw[t][:], psS[t % 2][:]).then_inc(raw_done, 1)

            def decays(i, layer, c, t):
                n = tile_no(i, layer, c, t)
                act.wait_ge(dist_done, n + 1)
                nc.scalar.activation(W[t][:], W[t][:], ACT.Ln, bias=tiny).then_inc(log_done, 1)
                act.wait_ge(log_done, n + 1)
                nc.scalar.activation(W[t][:], W[t][:], ACT.Exp, scale=0.5).then_inc(root_done, 1)
                act.wait_ge(root_done, n + 1)
                nc.scalar.activation(W[t][:], W[t][:], ACT.Exp, scale=-1.0).then_inc(te_done, 1)

            def probs(i, layer, c, t):
                n = tile_no(i, layer, c, t)
                act.wait_ge(logitsT_ready, n + 1)
                after(act, weighted_ready, n + 1 - 2)
                nc.scalar.activation(PT[t % 2][:].rearrange("p g q -> p (g q)"), psT[:], ACT.Exp).then_inc(probs_done, 1)

            def job(i, place, kind, layer, c, chunk):
                src = psJ[BANK[place]]
                mine = job_count(i, kind, layer, c, chunk)
                column = lambda n: cols[:, n, layer:layer + 1]
                if kind not in ("xT", "key", "value", "attT", "mean", "var", "ff1", "out"):
                    return
                act.wait_ge(ready[kind], mine)
                if kind == "xT":
                    after(act, done["proj"], job_count(i, "proj", layer, c - 1) if exists(i, c - 1) else 0)
                    nc.scalar.copy(xT[:, layer], src[:]).then_inc(done[kind], 1)
                elif kind == "key":
                    after(act, scores_ready, tile_no(i, layer, c - 1, TB) if exists(i, c - 1) else 0)
                    nc.scalar.activation(kh[:, layer], src[:], ACT.Identity, scale=0.5, bias=column(HKB)).then_inc(done[kind], 1)
                elif kind == "value":
                    after(act, weighted_ready, tile_no(i, layer, c - 1, TB) if exists(i, c - 1) else 0)
                    for e in range(2):
                        rows = slice(e * S, (e + 1) * S)
                        nc.scalar.copy(vx[layer][rows, :, :, e * DK:(e + 1) * DK],
                                       src[rows].rearrange("p (b g d) -> p b g d", b=BB, g=HP)).then_inc(done[kind], 1)
                elif kind == "attT":
                    after(act, ready["proj"], mine - 1)
                    nc.scalar.activation(attT[:], src[:], ACT.Identity, bias=column(VB)).then_inc(done[kind], 1)
                    if layer == 2:
                        act.wait_ge(done[kind], mine)
                        nc.scalar.copy(attT[:].rearrange("p (b q) -> p b q", b=BB)[:, :, 0:1],
                                       zeros[:, 0:BB].unsqueeze(2)).then_inc(padded, 1)
                elif kind == "mean":
                    after(act, ready["var"], mine - 1)
                    nc.scalar.activation(square[:], src[:], ACT.Square).then_inc(square_done, 1)
                elif kind == "var":
                    after(act, done["mean"], mine - 1)
                    nc.scalar.activation(rstd[:], src[:], ACT.Ln, bias=eps_ln).then_inc(done[kind], 1)
                    act.wait_ge(done[kind], mine)
                    nc.scalar.activation(rstd[:], rstd[:], ACT.Exp, scale=-0.5).then_inc(rstd_done, 1)
                elif kind == "ff1":
                    after(act, ready["ff2"], ffn_no(i, layer, c))
                    nc.scalar.activation(hT[:, chunk], src[:], ACT.Relu, bias=b1c[:, layer, chunk:chunk + 1]).then_inc(done[kind], 1)
                elif kind == "out":
                    after(act, stored, line(i, 16, 16 * c))
                    nc.scalar.copy(outb[:].rearrange("p t d -> p (t d)"), src[:]).then_inc(done[kind], 1)

            def affine(i, layer, c, which):
                act.wait_ge(done["mean"], norm_no(i, layer, c, which) + 1)
                gain, bias = (G1, B1) if which == 1 else (G2, B2)
                if (layer, which) == (1, 1):
                    dst = x1T
                    if exists(i, c - 1):
                        act.wait_ge(done["proj"], job_count(i, "proj", 2, c - 1))
                        act.wait_ge(ready["key"], job_count(i, "key", 2, c - 1))
                elif which == 1:
                    dst = xfT
                    after(act, done["ff2"], ffn_no(i, layer, c))
                elif layer == 0:
                    dst = yT
                    if exists(i, c - 1):
                        act.wait_ge(ready["value"], job_count(i, "value", 2, c - 1))
                else:
                    dst = outT
                    after(act, ready["out"], line(i, 1, c))
                nc.scalar.activation(dst[:], normed[:], ACT.Identity, scale=cols[:, gain, layer:layer + 1],
                                     bias=cols[:, bias, layer:layer + 1]).then_inc(affine_done, 1)

            def stage(i, r, lag, work):
                layer, c, t = at_step(r - lag)
                if exists(i, c):
                    work(i, layer, c, t)

            def jobs(i, part):
                for _, kind, layer, c, which in jobs_in(part, 3):
                    if kind == "var" and exists(i, c):
                        affine(i, layer, c, which)
                for one_job in jobs_in(part, 1):
                    if exists(i, one_job[3]):
                        job(i, *one_job)

            def step(i, r):
                stage(i, r, 2, decays)
                jobs(i, PARTS * r)
                stage(i, r, 3, probs)
                stage(i, r, 0, exp1)
                jobs(i, PARTS * r + 1)
                stage(i, r, 0, keep_raw)
                jobs(i, PARTS * r + 2)

            rounds(act, step)

        @block.vector
        def _(dve):
            count = [0]

            def setup(ins):
                count[0] += 1
                ins.then_inc(setup_dve, 1)
                dve.wait_ge(setup_dve, count[0])

            dve.wait_ge(setup_act, 2)
            flat = lambda a: a.rearrange("p l h s c -> p (l h s c)")
            setup(nc.vector.tensor_tensor(flat(al), flat(al), flat(ge), ALU.subtract))
            dve.wait_ge(setup_pool, 2)
            setup(nc.vector.tensor_tensor(hidden[:, :, :, S:SKEW].rearrange("p l h s -> p (l h) s"),
                                          al[:, :, :, :, 0].rearrange("p l h s -> p (l h) s"),
                                          al[:, :, :, :, 1].rearrange("p l h s -> p (l h) s"), ALU.is_ge))
            setup(nc.vector.tensor_scalar(hidden[:].rearrange("p l h u -> p (l h u)"),
                                          hidden[:].rearrange("p l h u -> p (l h u)"), NEG, None, ALU.mult))
            dve.wait_ge(setup_act, 4)
            setup(nc.vector.scalar_tensor_tensor(gam[:, 4, :], gam[:, 0, :], 0.0, gam[:, 3, :], ALU.max, ALU.add))
            setup(nc.vector.tensor_tensor(gam[:, 4, :], gam[:, 4, :], gam[:, 4, :], ALU.mult))
            dve.wait_ge(setup_pool, 5)
            for l in range(L):
                setup(nc.vector.tensor_tensor(per_head(decay[:, l]), per_head(dist_ij[:]),
                                              over_keys(gam[:, 4, l * H:(l + 1) * H]), ALU.mult))
            dve.wait_ge(wT_done, 1)
            setup(nc.vector.tensor_scalar(cols[:, HKB, :], cols[:, HKB, :], 0.5, None, ALU.mult))
            dve.wait_ge(wT_done, 9)
            for n in range(L):
                setup(nc.vector.memset(kx[n][:].rearrange("p h t -> p (h t)"), 0.0))
                setup(nc.vector.memset(vx[n][:].rearrange("p b g c -> p (b g c)"), 0.0))
                for e in range(2):
                    setup(nc.vector.memset(vx[n][e * S:(e + 1) * S, :, :, 2 * DK + e:2 * DK + e + 1], 1.0))
            for t in range(TB):
                setup(nc.vector.memset(E[t][:, H * S:H * S + 1], 0.0))
            assert count[0] == SETUP_DVE, count[0]
            dve.wait_ge(setup_pool, SETUP_POOL)

            def over(n, k):
                return n * 3 + k

            def max1(i, layer, c, t):
                dve.wait_ge(scores_ready, tile_no(i, layer, c, t) + 1)
                nc.vector.tensor_reduce(neg1[:, t], per_head(psS[t % 2][:]), AX_X, ALU.max, negate=True).then_inc(max1_done, 1)

            def shift1(i, layer, c, t):
                n = tile_no(i, layer, c, t)
                dve.wait_ge(max1_done, n + 1)
                after(dve, tree_step, over(n - TB, 1))
                nc.vector.tensor_tensor(per_head(E[t][:, 0:H * S]), per_head(psS[t % 2][:]), over_keys(neg1[:, t]),
                                        ALU.add).then_inc(shift1_done, 1)

            def scan(i, layer, c, t):
                n = tile_no(i, layer, c, t)
                dve.wait_ge(exp1_done, n + 1)
                after(dve, logitsT_ready, n + 1 - TB)
                nc.vector.tensor_tensor_scan(W[t][:, ::-1], E[t][:, 1:H * S + 1][:, ::-1], keep[:, BMASK[layer]][:, ::-1],
                                             0.0, ALU.add, ALU.mult).then_inc(scan_done, 1)

            def den1_of(i, layer, c, t):
                dve.wait_ge(tree_step, over(tile_no(i, layer, c, t), 3))
                nc.vector.tensor_reduce(den1[:, t], tree[2][:], AX_X, ALU.add).then_inc(den1_done, 1)

            def rden1_of(i, layer, c, t):
                dve.wait_ge(den1_done, tile_no(i, layer, c, t) + 1)
                nc.vector.reciprocal(rden1[:, t], den1[:, t]).then_inc(rden1_done, 1)

            def logits(i, layer, c, t):
                n = tile_no(i, layer, c, t)
                dve.wait_ge(te_done, n + 1)
                dve.wait_ge(raw_done, n + 1)
                nc.vector.scalar_tensor_tensor(W[t][:], W[t][:], TE_MIN, raw[t][:], ALU.max, ALU.mult).then_inc(logits_done, 1)

            def max2(i, layer, c, t):
                dve.wait_ge(logits_done, tile_no(i, layer, c, t) + 1)
                nc.vector.tensor_reduce(neg2[:, t], per_head(W[t][:]), AX_X, ALU.max, negate=True).then_inc(max2_done, 1)

            def shift2(i, layer, c, t):
                dve.wait_ge(max2_done, tile_no(i, layer, c, t) + 1)
                nc.vector.tensor_tensor(per_head(W[t][:]), per_head(W[t][:]), over_keys(neg2[:, t]), ALU.add).then_inc(shift2_done, 1)

            att_parts = psO[:, 0:HP * VW].rearrange("p (g c) -> p g c", g=HP)

            def rden2_of(i, layer, c, t):
                dve.wait_ge(weighted_ready, tile_no(i, layer, c, t) + 1)
                nc.vector.reciprocal(rden2[:, t], att_parts[:, :, 2 * DK:VW]).then_inc(rden2_done, 1)

            def attend(i, layer, c, t):
                dve.wait_ge(rden2_done, tile_no(i, layer, c, t) + 1)
                if t == 0:
                    after(dve, ready["attT"], job_count(i, "attT", layer, c - 1) if exists(i, c - 1) else 0)
                nc.vector.tensor_tensor(att[:, layer, t].rearrange("p (g e d) -> p g e d", g=HP, e=2),
                                        att_parts[:, :, 0:2 * DK].rearrange("p g (e d) -> p g e d", e=2),
                                        rden2[:, t].unsqueeze(3).to_broadcast([P, HP, 2, DK]), ALU.mult).then_inc(att_done, 1)

            def scale(i, place, layer, c, which):
                n = norm_no(i, layer, c, which)
                centred = psJ[BANK[ORDER.index(("mean",) + ORDER[place][1:])]]
                dve.wait_ge(rstd_done, n + 1)
                after(dve, affine_done, n)
                nc.vector.tensor_tensor(normed[:], centred[:], rstd[:], ALU.mult).then_inc(done["mean"], 1)

            def job(i, place, kind, layer, c, chunk):
                src = psJ[BANK[place]]
                mine = job_count(i, kind, layer, c, chunk)
                column = lambda n: cols[:, n, layer:layer + 1]
                if kind == "proj":
                    dve.wait_ge(ready[kind], mine)
                    after(dve, ready["mean"], last_mean(i, place, 1, layer, c))
                    residual = x1T[:] if layer == 2 else xT[:, layer]
                    nc.vector.scalar_tensor_tensor(zT[:], src[:], column(OB), residual, ALU.add, ALU.add).then_inc(done[kind], 1)
                elif kind == "ff2":
                    dve.wait_ge(ready[kind], mine)
                    after(dve, ready["mean"], last_mean(i, place, 2, layer, c))
                    nc.vector.scalar_tensor_tensor(rT[:], src[:], column(BF2), xfT[:], ALU.add, ALU.add).then_inc(done[kind], 1)

            def last_mean(i, place, which, layer, c):
                places = [job for job in ORDER if job[0] == "mean"]
                at = next(k for k, job in enumerate(places) if job[1] == layer and job[3] == which)
                k, turn, c0 = at, 0, c - places[at][2]
                while True:
                    k -= 1
                    if k < 0:
                        k, turn = len(places) - 1, turn - 1
                    if isinstance(i, int) and i + c0 + turn < FIRST_ROUND:
                        return 0
                    _, l, own, w = places[k]
                    if w == which and exists(i, own + c0 + turn):
                        return norm_no(i, l, own + c0 + turn, w) + 1

            def stage(i, r, lag, *work):
                layer, c, t = at_step(r - lag)
                if exists(i, c):
                    for one in work:
                        one(i, layer, c, t)

            def jobs(i, part):
                for place, kind, layer, c, which in jobs_in(part, 2):
                    if kind == "var" and exists(i, c):
                        scale(i, place, layer, c, which)
                for one in jobs_in(part, 1):
                    if exists(i, one[3]):
                        job(i, *one)

            def step(i, r):
                stage(i, r, 0, max1)
                stage(i, r, 4, rden2_of)
                stage(i, r, 0, shift1)
                stage(i, r, 4, attend)
                jobs(i, PARTS * r)
                stage(i, r, 1, scan)
                jobs(i, PARTS * r + 1)
                stage(i, r, 2, logits)
                stage(i, r, 1, den1_of)
                stage(i, r, 2, max2)
                stage(i, r, 1, rden1_of)
                stage(i, r, 2, shift2)
                jobs(i, PARTS * r + 2)

            rounds(dve, step)

        @block.gpsimd
        def _(pool):
            count = [0]

            def setup(ins):
                count[0] += 1
                ins.then_inc(setup_pool, 1)
                pool.wait_ge(setup_pool, count[0])

            for n, value in enumerate((TINY, EPS_LN, EPS_LOG, 1.0)):
                last = nc.gpsimd.memset(small[:, n:n + 1], value)
            setup(last)
            setup(nc.gpsimd.memset(hidden[:, :, :, 0:S], 0.0))
            setup(nc.gpsimd.memset(identf[:], 0.0))
            setup(nc.gpsimd.affine_select(out=identf[:], in_=identf[:], compare_op=ALU.not_equal, fill=1.0, base=0,
                                          pattern=[[-1, P]], channel_multiplier=1))
            for n in range(BT):
                last = nc.gpsimd.iota(per_head(dist_ij[n * S:(n + 1) * S]), pattern=[[0, H], [-1, S]], base=0,
                                      channel_multiplier=1, allow_small_or_imprecise_dtypes=True)
            setup(last)
            setup(nc.gpsimd.memset(identb[:], 0.0))
            setup(nc.gpsimd.affine_select(out=identb[:], in_=identb[:], compare_op=ALU.not_equal, fill=1.0, base=0,
                                          pattern=[[-1, P]], channel_multiplier=1))
            setup(nc.gpsimd.memset(zeros[:], 0.0))
            setup(nc.gpsimd.memset(average[:], 1.0 / D))
            setup(nc.gpsimd.tensor_tensor(centre[:], identf[:], average[:], ALU.subtract))
            for m in range(2):
                for n in range(BT):
                    rows = slice(n * S, (n + 1) * S)
                    setup(nc.gpsimd.affine_select(out=per_head(causal_bias[rows, m]), in_=per_head(zeros[rows]), compare_op=ALU.is_gt,
                                                  fill=NEG, base=m, pattern=[[0, H], [-1, S]], channel_multiplier=1))
                    setup(nc.gpsimd.affine_select(out=per_head(keep[rows, m]), in_=per_head(zeros[rows]), compare_op=ALU.is_ge,
                                                  fill=1.0, base=1 - m, pattern=[[0, H], [1, S]], channel_multiplier=-1))
            for m in range(2):
                setup(nc.gpsimd.memset(per_head(keep[:, m])[:, :, S - 1:S], 0.0))
            pool.wait_ge(skew_read, 16 * BT)
            for l in range(L):
                for n in range(BT):
                    rows = slice(n * S, (n + 1) * S)
                    setup(nc.gpsimd.affine_select(out=per_head(mask_bias[rows, l]), in_=shifted_mask[rows, l], compare_op=ALU.is_ge,
                                                  fill=0.0, base=-BMASK[l], pattern=[[0, H], [1, S]], channel_multiplier=-1))
            assert count[0] == SETUP_POOL, count[0]

            def sums(i, layer, c, t):
                n = tile_no(i, layer, c, t)
                pool.wait_ge(exp1_done, n + 1)
                src = per_head(E[t][:, 0:H * S])
                for k, half in enumerate((32, 16, 8)):
                    after(pool, tree_step, n * 3 + k)
                    if k == 2:
                        after(pool, den1_done, n)
                    nc.gpsimd.tensor_tensor(tree[k][:], src[:, :, 0:half], src[:, :, half:2 * half], ALU.add).then_inc(tree_step, 1)
                    src = tree[k][:]

            def distances(i, layer, c, t):
                n = tile_no(i, layer, c, t)
                pool.wait_ge(scan_done, n + 1)
                nc.gpsimd.tensor_tensor(W[t][:], W[t][:], decay[:, layer], ALU.mult).then_inc(decay_done, 1)
                pool.wait_ge(decay_done, n + 1)
                pool.wait_ge(rden1_done, n + 1)
                nc.gpsimd.tensor_tensor(per_head(W[t][:]), per_head(W[t][:]), over_keys(rden1[:, t]), ALU.mult).then_inc(dist_done, 1)

            def step(i, r):
                layer, c, t = at_step(r - 1)
                if exists(i, c):
                    sums(i, layer, c, t)
                    distances(i, layer, c, t)

            rounds(pool, step)


WEIGHT_LOADS = 3 + 4 + 8 + 1
SETUP_DVE = 9 + 4 * L + TB
SETUP_POOL = 10 + 8 + 2 + 2 * L


_INS = ["x", "ctx_1024", "L0_xattn_kW", "L0_xattn_kb", "L0_xattn_vW", "L0_xattn_vb", "L0_xattn_oW", "L0_xattn_ob",
        "L0_xattn_gammas", "L0_xattn_alphas", "L0_xattn_ln1_g", "L0_xattn_ln1_b", "L0_xattn_w1", "L0_xattn_b1",
        "L0_xattn_w2", "L0_xattn_b2", "L0_xattn_ln2_g", "L0_xattn_ln2_b", "L0_xattn_gumbel_E"]


def kernel(**inputs):
    import numpy as _np
    import concourse.bacc as _bacc
    from concourse import mybir as _mybir
    from concourse.bass_utils import run_bass_kernel_spmd as _run

    nc = _bacc.Bacc("TRN2", target_bir_lowering=False, num_devices=1)
    arrays, args = {}, []
    for name in _INS:
        a = _np.ascontiguousarray(inputs[name])
        arrays[f"in_{name}"] = a
        args.append(nc.dram_tensor(f"in_{name}", a.shape, _mybir.dt.from_np(a.dtype), kind="ExternalInput").ap())
    out = nc.dram_tensor("out_0", (B, S, D), F32, kind="ExternalOutput").ap()
    build(nc, *args, out)
    r = _run(nc, [arrays], core_ids=[0])
    return r.results[0]["out_0"]
```

```python
from contextlib import ExitStack

import concourse.bass as bass
from concourse import mybir

ALU = mybir.AluOpType
ACT = mybir.ActivationFunctionType
AX_X = mybir.AxisListType.X
F32 = mybir.dt.float32
BF16 = mybir.dt.bfloat16

P = 128
B, S, D, H, DFF, L = 128, 64, 128, 8, 512, 3
DK = D // H
BT = P // S
TB = 4
GROUPS = B // (BT * TB)
TOK = TB * P
BB = BT * TB
HP = H // 2
VW = 2 * DK + 2
FC = DFF // P
STEPS = L * TB
NEG = -1e32
TINY = 1e-30
EPS_LN = 1e-5
EPS_LOG = 1e-5
TE_MIN = 1e-5
BMASK = (1, 1, 0)
SKEW = 2 * S

PARTS = 3
SCHEDULE = {
    1: [("acc", 0, -1, 0), ("acc", 0, -1, 1), ("acc", 0, -1, 2)], 2: [("ff2", 0, -1, 0)], 3: [("attT", 1, -1, 0)],
    4: [("var", 0, -1, 2)], 5: [("xT", 1, 0, 0), ("proj", 1, -1, 0)], 6: [("key", 1, 0, 0)],
    8: [("value", 0, 0, 0), ("value", 1, 0, 0)], 9: [("var", 1, -1, 1), ("attT", 2, -2, 0)], 10: [("proj", 2, -2, 0)],
    13: [("var", 2, -2, 1)], 16: [("key", 2, -1, 0)], 17: [("value", 2, -1, 0), ("ff1", 2, -2, 0)],
    19: [("acc", 2, -2, 0), ("ff1", 2, -2, 1)], 20: [("ff1", 2, -2, 2)], 21: [("ff1", 2, -2, 3)],
    22: [("acc", 2, -2, 1)], 23: [("acc", 2, -2, 2)], 24: [("ff2", 2, -2, 0)],
    25: [("attT", 0, 0, 0), ("var", 2, -2, 2)], 26: [("proj", 0, 0, 0)], 27: [("xT", 0, 1, 0)],
    28: [("var", 0, 0, 1), ("key", 0, 1, 0)], 32: [("ff1", 0, 0, 0)], 33: [("out", 2, -2, 0), ("ff1", 0, 0, 1)],
    34: [("ff1", 0, 0, 2), ("ff1", 0, 0, 3)],
}
NORMED = ("proj", "ff2")
ORDER = [job for part in sorted(SCHEDULE) for job in SCHEDULE[part]]
JOB_BANKS = 4


def spread_banks():
    left, banks = [0] * JOB_BANKS, []
    for turn in range(2):
        banks = []
        for part in sorted(SCHEDULE):
            for kind, layer, c, chunk in SCHEDULE[part]:
                if kind == "ff2" or (kind == "acc" and chunk > 0):
                    banks.append(banks[ORDER.index(("acc", layer, c, 0))])
                    continue
                life = 1.5
                if kind in ("proj", "acc"):
                    which = 1 if kind == "proj" else 2
                    var = next(p for p, jobs in SCHEDULE.items() for j in jobs if j[:2] == ("var", layer) and j[3] == which)
                    life = (var - part) % (PARTS * STEPS) + 2.5
                banks.append(min(range(JOB_BANKS), key=lambda n: left[n]))
                left[banks[-1]] = turn * PARTS * STEPS + part + life + 0.01 * len(banks)
    return banks


BANK = spread_banks()
OLDEST = min(job[2] for job in ORDER)
FIRST_ROUND, LOOP_FROM, LOOP_TO, LAST_ROUND = -1, -OLDEST, GROUPS - 2, GROUPS - 1 - OLDEST


def exists(i, c):
    return not isinstance(i, int) or 0 <= i + c < GROUPS


def line(i, a, b):
    return i * a + b


def block_no(i, layer, c):
    if isinstance(i, int):
        k = i + c
        return 2 * min(k + 2, GROUPS) + k if layer == 2 else 2 * k + max(k - 1, 0) + layer
    return line(i, 3, 3 * c + (4 if layer == 2 else layer - 1))


def tile_no(i, layer, c, t):
    if isinstance(i, int):
        return TB * block_no(i, layer, c) + t
    return line(i, 3 * TB, TB * (3 * c + (4 if layer == 2 else layer - 1)) + t)


def ffn_no(i, layer, c):
    if isinstance(i, int):
        k = i + c
        return min(k + 2, GROUPS) + k if layer == 2 else k + max(k - 1, 0)
    return line(i, 2, 2 * c + (2 if layer == 2 else -1))


def norm_no(i, layer, c, which):
    norms = [(n, job) for n, job in enumerate(ORDER) if job[0] in NORMED]
    place, own = next((n, job[2]) for n, job in norms if job[:2] == (NORMED[which - 1], layer))
    i, past = i + (c - own), LOOP_FROM

    def before(last):
        return sum(exists(n, job[2]) and (n < last or j < place)
                   for n in range(FIRST_ROUND, last + 1) for j, job in norms)

    return before(i) if isinstance(i, int) else line(i, len(norms), before(past) - past * len(norms))


def job_count(i, kind, layer, c, chunk=0):
    if kind == "ff1":
        if isinstance(i, int):
            return FC * ffn_no(i, layer, c) + chunk + 1
        return line(i, 2 * FC, FC * (2 * c + (2 if layer == 2 else -1)) + chunk + 1)
    if kind in ("acc", "ff2"):
        return ffn_no(i, layer, c) + 1
    if kind == "xT":
        return line(i, 2, 2 * c + layer + 1)
    if kind == "out":
        return line(i, 1, c + 1)
    if kind == "var":
        return norm_no(i, layer, c, chunk) + 1
    return block_no(i, layer, c) + 1


def after(eng, sem, count):
    if not isinstance(count, int) or count > 0:
        eng.wait_ge(sem, count)


def jobs_in(part, late=0):
    past, part = divmod(part - late, PARTS * STEPS)
    return [(ORDER.index(j), j[0], j[1], j[2] + past, j[3]) for j in SCHEDULE.get(part, [])]


def at_step(r):
    d, r = divmod(r, STEPS)
    layer = r // TB
    return layer, d - (layer == 2), r % TB


def rounds(eng, step):
    for i in range(FIRST_ROUND, LOOP_FROM):
        for r in range(STEPS):
            step(i, r)
    with eng.Fori(LOOP_FROM, LOOP_TO) as i:
        for r in range(STEPS):
            step(i, r)
    for i in range(LOOP_TO, LAST_ROUND + 1):
        for r in range(STEPS):
            step(i, r)


def build(nc, x, ctx, kW, kb, vW, vb, oW, ob, gammas, alphas, ln1_g, ln1_b, w1, b1, w2, b2, ln2_g, ln2_b,
          gumbel, out):
    with ExitStack() as stack:
        def sb(name, shape, dt=F32):
            return stack.enter_context(nc.sbuf_tensor(name, shape, dt))

        def sem(name):
            return stack.enter_context(nc.semaphore(name))

        psS = [stack.enter_context(nc.psum_tensor(f"psS{n}", [P, TOK], F32)) for n in range(2)]
        psT = stack.enter_context(nc.psum_tensor("psT", [P, TOK], F32))
        psO = stack.enter_context(nc.psum_tensor("psO", [P, TOK], F32))
        psJ = [stack.enter_context(nc.psum_tensor(f"psJ{n}", [P, TOK], F32)) for n in range(JOB_BANKS)]

        identf = sb("identf", [P, P])
        identb = sb("identb", [P, P], BF16)
        mask_bias = sb("mask_bias", [P, L, H * S], BF16)
        causal_bias = sb("causal_bias", [P, 2, H * S], BF16)
        keep = sb("keep", [P, 2, H * S])
        decay = sb("decay", [P, L, H * S])
        kWT = sb("kWT", [P, L, D])
        vWT = sb("vWT", [P, L, D])
        oWT = sb("oWT", [P, L, D])
        w1T = sb("w1T", [P, 2, DFF])
        w2T = sb("w2T", [P, 2, FC, D])
        cols = sb("cols", [P, 8, L])
        HKB, VB, OB, G1, B1, BF2, G2, B2 = range(8)
        b1c = sb("b1c", [P, L, FC])
        vectors = sb("vectors", [(8 + FC) * L, D])
        small = sb("small", [P, 4])
        xin = sb("xin", [P, 2, TB, D])
        xT = sb("xT", [P, 2, TOK])
        x1T = sb("x1T", [P, TOK])
        xfT = sb("xfT", [P, TOK])
        yT = sb("yT", [P, TOK])
        kh = sb("kh", [P, L, TOK])
        kx = [sb(f"kx{n}", [P, H, TOK]) for n in range(L)]
        vx = [sb(f"vx{n}", [P, BB, HP, VW]) for n in range(L)]
        E = [sb(f"E{n}", [P, H * S + 1]) for n in range(TB)]
        W = [sb(f"W{n}", [P, H * S]) for n in range(TB)]
        raw = [sb(f"raw{n}", [P, H * S]) for n in range(TB)]
        PT = [sb(f"PT{n}", [P, HP, P]) for n in range(2)]
        tree = [sb(f"tree{n}", [P, H, n]) for n in (32, 16, 8)]
        neg1 = sb("neg1", [P, TB, H])
        den1 = sb("den1", [P, TB, H])
        rden1 = sb("rden1", [P, TB, H])
        neg2 = sb("neg2", [P, TB, H])
        rden2 = sb("rden2", [P, TB, HP, 2])
        att = sb("att", [P, L, TB, D])
        attT = sb("attT", [P, TOK])
        square = sb("square", [P, TOK])
        rstd = sb("rstd", [P, TOK])
        normed = sb("normed", [P, TOK])
        outT = sb("outT", [P, TOK])
        centre = sb("centre", [P, P])
        average = sb("average", [P, P])
        hT = sb("hT", [P, FC, TOK])
        outb = sb("outb", [P, TB, D])
        flat = kx[2][:].rearrange("p h t -> p (h t)")
        n_nat, n_w = 3 * L * D, 2 * DFF
        natural = flat[:, 0:n_nat].rearrange("p (n l d) -> p n l d", n=3, l=L)
        w1n = flat[:, n_nat:n_nat + n_w].rearrange("p (n c d) -> p n c d", n=2, c=FC)
        w2n = flat[:, n_nat + n_w:n_nat + 2 * n_w].rearrange("p (n f) -> p n f", n=2)
        al = sb("al", [L * H, S, 2])
        ge = sb("ge", [L * H, S, 2])
        hidden = sb("hidden", [L * H, SKEW])
        shifted_mask = hT[:].rearrange("p c t -> p (c t)")[:, 0:L * H * S].rearrange("p (l h s) -> p l h s", l=L, h=H)
        gam = sb("gam", [P, 5, L * H])
        zeros = sb("zeros", [P, H * S])
        dist_ij = sb("dist_ij", [P, H * S])
        skew = nc.dram_tensor("skew", [L * H, S * (SKEW + 1)], F32, kind="Internal").ap()

        loaded = sem("loaded")
        gammas_loaded = sem("gammas_loaded")
        weights_loaded = sem("weights_loaded")
        setup_pool = sem("setup_pool")
        setup_act = sem("setup_act")
        setup_dve = sem("setup_dve")
        layer_zeroed = sem("layer_zeroed")
        mask_ready = sem("mask_ready")
        skew_written = sem("skew_written")
        skew_read = sem("skew_read")
        wT_ready = sem("wT_ready")
        wT_done = sem("wT_done")
        scores_ready = sem("scores_ready")
        max1_done = sem("max1_done")
        shift1_done = sem("shift1_done")
        exp1_done = sem("exp1_done")
        causal_ready = sem("causal_ready")
        raw_done = sem("raw_done")
        tree_step = sem("tree_step")
        den1_done = sem("den1_done")
        rden1_done = sem("rden1_done")
        scan_done = sem("scan_done")
        decay_done = sem("decay_done")
        dist_done = sem("dist_done")
        log_done = sem("log_done")
        root_done = sem("root_done")
        te_done = sem("te_done")
        logits_done = sem("logits_done")
        max2_done = sem("max2_done")
        shift2_done = sem("shift2_done")
        logitsT_ready = sem("logitsT_ready")
        probs_done = sem("probs_done")
        weighted_ready = sem("weighted_ready")
        rden2_done = sem("rden2_done")
        att_done = sem("att_done")
        kinds = ("xT", "key", "value", "attT", "proj", "var", "ff1", "ff2", "out")
        ready = {k: sem(f"{k}_ready") for k in kinds}
        done = {k: sem(f"{k}_done") for k in kinds}
        x_loaded = [sem(f"x_loaded{n}") for n in range(2)]
        kx_filled = [sem(f"kx_filled{n}") for n in range(L)]
        padded = sem("padded")
        scaled = sem("scaled")
        square_done = sem("square_done")
        rstd_done = sem("rstd_done")
        affine_done = sem("affine_done")
        stored = sem("stored")

        x_groups = [a.rearrange("(s t b) q d -> s (b q) t d", t=TB, b=BT) for a in (ctx, x)]
        out_groups = out.rearrange("(s t b) q d -> s (b q) t d", t=TB, b=BT)

        def first(i, c):
            return isinstance(i, int) and i + c == 0

        def per_head(ap):
            return ap.rearrange("p (h k) -> p h k", h=H)

        def over_keys(ap):
            return ap.unsqueeze(2).to_broadcast([P, H, S])

        def bank_free(eng, i, place):
            n, back = place, 0
            while not isinstance(i, int) or i + back >= FIRST_ROUND:
                n -= 1
                if n < 0:
                    n, back = len(ORDER) - 1, back - 1
                kind, layer, c, chunk = ORDER[n]
                if BANK[n] == BANK[place] and exists(i, c + back):
                    assert kind != "acc"
                    if kind in NORMED:
                        after(eng, scaled, norm_no(i, layer, c + back, 1 + NORMED.index(kind)) + 1)
                    else:
                        reads = BT * 2 if kind == "value" else 1
                        after(eng, done[kind], job_count(i, kind, layer, c + back, chunk) * reads)
                    return

        ffn = {0: 0, 2: 1}

        block = stack.enter_context(nc.Block())

        @block.sync
        def _(sp):
            sp.dma_start(ge[:], gumbel.rearrange("l h s c -> (l h) s c")).then_inc(loaded, 16)
            sp.dma_start(al[:], alphas.rearrange("l h s c -> (l h) s c")).then_inc(loaded, 16)
            for n, a in enumerate((kW, vW, oW)):
                sp.dma_start(natural[:, n], a.rearrange("l o i -> o l i")).then_inc(weights_loaded, 16)
            for n, l in enumerate((0, 2)):
                sp.dma_start(w1n[:, n], w1[l].rearrange("(c p) i -> p c i", p=P)).then_inc(weights_loaded, 16)
                sp.dma_start(w2n[:, n], w2[l]).then_inc(weights_loaded, 16)
            for n, a in enumerate((kb, vb, ob, ln1_g, ln1_b, b2, ln2_g, ln2_b)):
                sp.dma_start(vectors[n * L:(n + 1) * L, :], a).then_inc(weights_loaded, 16)
            sp.dma_start(vectors[8 * L:, :], b1.rearrange("l (c p) -> (l c) p", p=P)).then_inc(weights_loaded, 16)
            sp.dma_start(gam[:, 0, :], gammas.rearrange("l h a b -> (l h a b)").partition_broadcast(P)).then_inc(gammas_loaded, 16)

            def step(i, r):
                for part in range(PARTS * r, PARTS * r + PARTS):
                    for _, kind, layer, c, _ in jobs_in(part, 1):
                        if kind == "xT" and exists(i, c) and exists(i, c + 1):
                            sp.wait_ge(ready["xT"], job_count(i, "xT", layer, c))
                            sp.dma_start(xin[:, layer], x_groups[layer][i + (c + 1)]).then_inc(x_loaded[layer], 16)
                        if kind == "key" and exists(i, c):
                            sp.wait_ge(done["key"], job_count(i, "key", layer, c))
                            if first(i, c):
                                sp.wait_ge(layer_zeroed, layer + 1)
                            for h in range(H):
                                rows = slice(h * DK, (h + 1) * DK)
                                sp.dma_start(kx[layer][rows, h, :], kh[rows, layer, :]).then_inc(kx_filled[layer], 16)
                    for _, kind, layer, c, _ in jobs_in(part, 2):
                        if kind == "out" and exists(i, c):
                            sp.wait_ge(done["out"], line(i, 1, c + 1))
                            sp.dma_start(out_groups[i + c], outb[:]).then_inc(stored, 16)

            for layer in range(2):
                sp.dma_start(xin[:, layer], x_groups[layer][0]).then_inc(x_loaded[layer], 16)
            rounds(sp, step)
            sp.wait_ge(stored, 16 * GROUPS)

        @block.tensor
        def _(pe):
            def transposes(dst, parts, sem_):
                for n, src in enumerate(parts):
                    last = nc.tensor.transpose(dst[:, n * P:(n + 1) * P], src, identf[:])
                last.then_inc(sem_, 1)

            def centred_transposes(dst, parts):
                for n, src in enumerate(parts):
                    last = nc.tensor.matmul(dst[:, n * P:(n + 1) * P], src, centre[:], start=True, stop=True)
                last.then_inc(wT_ready, 1)

            pe.wait_ge(setup_pool, CENTRE_DONE)
            pe.wait_ge(weights_loaded, WEIGHT_LOADS * 16)
            rows = (8 + FC) * L
            nc.tensor.transpose(psT[:, 0:rows], vectors[:], identf[0:rows, 0:rows]).then_inc(wT_ready, 1)
            for n in range(2):
                transposes(psJ[n], [natural[:, n, l, :] for l in range(L)], wT_ready)
            centred_transposes(psJ[2], [natural[:, 2, l, :] for l in range(L)])
            for n in range(2):
                if n:
                    pe.wait_ge(wT_done, 4)
                transposes(psJ[3] if not n else psJ[0], [w1n[:, n, c, :] for c in range(FC)], wT_ready)
            for n in range(2):
                pe.wait_ge(wT_done, n + 5)
                centred_transposes(psJ[n + 1], [w2n[:, n, c * P:(c + 1) * P] for c in range(FC)])
            for n in (OB, BF2):
                last = nc.tensor.matmul(psT[:, n * L:(n + 1) * L], centre[:], cols[:, n, :], start=True, stop=True)
            last.then_inc(wT_ready, 1)
            pe.wait_ge(wT_done, WEIGHTS_DONE)

            def scores(i, layer, c, t):
                n = tile_no(i, layer, c, t)
                after(pe, raw_done, n + 1 - 2)
                if t == 0:
                    pe.wait_ge(done["key"], job_count(i, "key", layer, c))
                    pe.wait_ge(kx_filled[layer], line(i, 16 * H, 16 * H * (c + 1)))
                    if first(i, c):
                        pe.wait_ge(mask_ready, BT * (layer + 1))
                nc.tensor.matmul(psS[t % 2][:], identb[:], mask_bias[:, layer], start=True, stop=False, skip_group_check=True)
                for b in range(BT):
                    tok = slice((t * BT + b) * S, (t * BT + b + 1) * S)
                    last = nc.tensor.matmul(psS[t % 2][b * S:(b + 1) * S, :], kh[:, layer, tok], kx[layer][:, :, tok],
                                            start=False, stop=True, skip_group_check=True)
                last.then_inc(scores_ready, 1)

            def causal(i, layer, c, t):
                n = tile_no(i, layer, c, t)
                pe.wait_ge(shift1_done, n + 1)
                nc.tensor.matmul(psS[t % 2][:], identb[:], causal_bias[:, BMASK[layer]], start=False, stop=True,
                                 skip_group_check=True).then_inc(causal_ready, 1)

            def logitsT(i, layer, c, t):
                n = tile_no(i, layer, c, t)
                after(pe, probs_done, n)
                pe.wait_ge(shift2_done, n + 1)
                transposes(psT, [W[t][:, g * P:(g + 1) * P] for g in range(HP)], logitsT_ready)

            def weighted(i, layer, c, t):
                n = tile_no(i, layer, c, t)
                after(pe, att_done, n)
                if t == 0:
                    pe.wait_ge(done["value"], job_count(i, "value", layer, c) * BT * 2)
                pe.wait_ge(probs_done, n + 1)
                for b in range(BT):
                    for g in range(HP):
                        last = nc.tensor.matmul(psO[b * S:(b + 1) * S, g * VW:(g + 1) * VW],
                                                PT[t % 2][:, g, b * S:(b + 1) * S], vx[layer][:, t * BT + b, g, :],
                                                start=True, stop=True)
                last.then_inc(weighted_ready, 1)

            def job(i, place, kind, layer, c, chunk):
                dst = psJ[BANK[place]]
                if kind != "ff2" and (kind != "acc" or chunk == 0):
                    bank_free(pe, i, place)
                count = lambda k, l=layer, cc=c: job_count(i, k, l, cc)
                if kind == "xT":
                    pe.wait_ge(x_loaded[layer], line(i, 16, 16 * (c + 1)))
                    transposes(dst, [xin[:, layer, t, :] for t in range(TB)], ready[kind])
                elif kind == "key":
                    if layer == 2:
                        pe.wait_ge(affine_done, norm_no(i, 1, c, 1) + 1)
                        src = x1T[:]
                    else:
                        pe.wait_ge(done["xT"], count("xT"))
                        src = xT[:, layer]
                    nc.tensor.matmul(dst[:], kWT[:, layer], src, start=True, stop=True).then_inc(ready[kind], 1)
                elif kind == "value":
                    if layer == 2:
                        pe.wait_ge(affine_done, norm_no(i, 0, c, 2) + 1)
                        src = yT
                    else:
                        src = xT[:, layer]
                    for t in range(TB):
                        last = nc.tensor.matmul(dst[:, t * P:(t + 1) * P], src[:, t * P:(t + 1) * P], vWT[:, layer],
                                                start=True, stop=True)
                    last.then_inc(ready[kind], 1)
                elif kind == "attT":
                    pe.wait_ge(att_done, tile_no(i, layer, c, TB))
                    transposes(dst, [att[:, layer, t, :] for t in range(TB)], ready[kind])
                elif kind == "proj":
                    nc.tensor.matmul(dst[:], centre[:], x1T[:] if layer == 2 else xT[:, layer], start=True, stop=False)
                    pe.wait_ge(done["attT"], count("attT"))
                    if layer == 2:
                        pe.wait_ge(padded, line(i, 1, c + 1))
                    nc.tensor.matmul(dst[:], oWT[:, layer], attT[:], start=False, stop=True).then_inc(ready[kind], 1)
                elif kind == "var":
                    pe.wait_ge(square_done, job_count(i, kind, layer, c, chunk))
                    nc.tensor.matmul(dst[:], average[:], square[:], start=True, stop=True).then_inc(ready[kind], 1)
                elif kind == "ff1":
                    pe.wait_ge(affine_done, norm_no(i, layer, c, 1) + 1)
                    nc.tensor.matmul(dst[:], w1T[:, ffn[layer], chunk * P:(chunk + 1) * P], xfT[:],
                                     start=True, stop=True).then_inc(ready[kind], 1)
                elif kind in ("acc", "ff2"):
                    if kind == "ff2":
                        chunk = FC - 1
                    if chunk == 0:
                        nc.tensor.matmul(dst[:], centre[:], xfT[:], start=True, stop=False)
                    pe.wait_ge(done["ff1"], job_count(i, "ff1", layer, c, chunk))
                    last = nc.tensor.matmul(dst[:], w2T[:, ffn[layer], chunk, :], hT[:, chunk, :],
                                            start=False, stop=(kind == "ff2"))
                    if kind == "ff2":
                        last.then_inc(ready[kind], 1)
                elif kind == "out":
                    pe.wait_ge(affine_done, norm_no(i, layer, c, 2) + 1)
                    transposes(dst, [outT[:, t * P:(t + 1) * P] for t in range(TB)], ready[kind])

            def stage(i, r, lag, work):
                layer, c, t = at_step(r - lag)
                if exists(i, c):
                    work(i, layer, c, t)

            def jobs(i, part):
                for one in jobs_in(part):
                    if exists(i, one[3]):
                        job(i, *one)

            def step(i, r):
                jobs(i, PARTS * r)
                stage(i, r, 3, logitsT)
                jobs(i, PARTS * r + 1)
                stage(i, r, -1, scores)
                stage(i, r, 0, causal)
                jobs(i, PARTS * r + 2)
                stage(i, r, 3, weighted)

            rounds(pe, step)

        @block.scalar
        def _(act):
            tiny, eps_log, one, eps_ln = (small[:, n:n + 1] for n in range(4))
            nc.scalar.preload_act_table_set("natural_log_exp_and_others")
            act.wait_ge(setup_pool, 1)
            act.wait_ge(loaded, 32)
            nc.scalar.activation(ge[:].rearrange("p s c -> p (s c)"), ge[:].rearrange("p s c -> p (s c)"),
                                 ACT.Ln, bias=eps_log[0:L * H]).then_inc(setup_act, 1)
            act.wait_ge(setup_dve, MASK_ROWS)
            nc.scalar.dma_start(bass.AP(skew.tensor, 0, [[S * (SKEW + 1), L * H], [SKEW + 1, S], [1, SKEW]]),
                                hidden[:].unsqueeze(1).to_broadcast([L * H, S, SKEW])).then_inc(skew_written, 16)
            act.wait_ge(gammas_loaded, 16)
            nc.scalar.activation(gam[:, 1, :], gam[:, 0, :], ACT.Abs).then_inc(setup_act, 1)
            act.wait_ge(setup_act, 2)
            nc.scalar.activation(gam[:, 2, :], gam[:, 1, :], ACT.Exp, scale=-1.0).then_inc(setup_act, 1)
            act.wait_ge(setup_act, 3)
            nc.scalar.activation(gam[:, 3, :], gam[:, 2, :], ACT.Ln, bias=one).then_inc(setup_act, 1)
            act.wait_ge(skew_written, 16)
            for n in range(BT):
                nc.scalar.dma_start(shifted_mask[n * S:(n + 1) * S].rearrange("p l h k -> p (l h) k"),
                                    bass.AP(skew.tensor, S, [[SKEW, S], [S * (SKEW + 1), L * H], [1, S]])).then_inc(skew_read, 16)
            act.wait_ge(wT_ready, 1)
            nc.scalar.mul(cols[:, HKB, :], psT[:, HKB * L:(HKB + 1) * L], 0.5).then_inc(wT_done, 1)
            targets = [(cols[:, VB:, :].rearrange("p n l -> p (n l)"), psT[:, VB * L:8 * L]),
                       (b1c[:].rearrange("p l c -> p (l c)"), psT[:, 8 * L:(8 + FC) * L]),
                       (kWT[:].rearrange("p l d -> p (l d)"), psJ[0][:, 0:L * D]), (vWT[:].rearrange("p l d -> p (l d)"), psJ[1][:, 0:L * D]),
                       (oWT[:].rearrange("p l d -> p (l d)"), psJ[2][:, 0:L * D]), (w1T[:, 0], psJ[3][:]), (w1T[:, 1], psJ[0][:]),
                       (w2T[:, 0].rearrange("p c d -> p (c d)"), psJ[1][:]), (w2T[:, 1].rearrange("p c d -> p (c d)"), psJ[2][:])]
            for n, (dst, src) in enumerate(targets):
                act.wait_ge(wT_ready, max(n, 1))
                nc.scalar.copy(dst, src).then_inc(wT_done, 1)
            act.wait_ge(wT_ready, 9)
            for n in (OB, BF2):
                nc.scalar.copy(cols[:, n, :], psT[:, n * L:(n + 1) * L]).then_inc(wT_done, 1)
            act.wait_ge(wT_done, WT_DONE)

            def exp1(i, layer, c, t):
                n = tile_no(i, layer, c, t)
                act.wait_ge(shift1_done, n + 1)
                nc.scalar.activation(E[t][:, 0:H * S], E[t][:, 0:H * S], ACT.Exp).then_inc(exp1_done, 1)

            def keep_raw(i, layer, c, t):
                n = tile_no(i, layer, c, t)
                act.wait_ge(causal_ready, n + 1)
                after(act, logits_done, n + 1 - TB)
                nc.scalar.copy(raw[t][:], psS[t % 2][:]).then_inc(raw_done, 1)

            def logs(i, layer, c, t):
                n = tile_no(i, layer, c, t)
                act.wait_ge(dist_done, n + 1)
                nc.scalar.activation(W[t][:], W[t][:], ACT.Ln, bias=tiny).then_inc(log_done, 1)

            def roots(i, layer, c, t):
                n = tile_no(i, layer, c, t)
                act.wait_ge(log_done, n + 1)
                nc.scalar.activation(W[t][:], W[t][:], ACT.Exp, scale=0.5).then_inc(root_done, 1)

            def decays(i, layer, c, t):
                n = tile_no(i, layer, c, t)
                act.wait_ge(root_done, n + 1)
                nc.scalar.activation(W[t][:], W[t][:], ACT.Exp, scale=-1.0).then_inc(te_done, 1)

            def probs(i, layer, c, t):
                n = tile_no(i, layer, c, t)
                act.wait_ge(logitsT_ready, n + 1)
                after(act, weighted_ready, n + 1 - 2)
                nc.scalar.activation(PT[t % 2][:].rearrange("p g q -> p (g q)"), psT[:], ACT.Exp).then_inc(probs_done, 1)

            def job(i, place, kind, layer, c, chunk):
                src = psJ[BANK[place]]
                mine = job_count(i, kind, layer, c, chunk)
                column = lambda n: cols[:, n, layer:layer + 1]
                if kind == "acc":
                    return
                act.wait_ge(ready[kind], mine)
                if kind == "xT":
                    after(act, ready["proj"], job_count(i, "proj", layer, c - 1) if exists(i, c - 1) else 0)
                    nc.scalar.copy(xT[:, layer], src[:]).then_inc(done[kind], 1)
                elif kind == "key":
                    after(act, scores_ready, tile_no(i, layer, c - 1, TB) if exists(i, c - 1) else 0)
                    nc.scalar.activation(kh[:, layer], src[:], ACT.Identity, scale=0.5, bias=column(HKB)).then_inc(done[kind], 1)
                elif kind == "value":
                    after(act, weighted_ready, tile_no(i, layer, c - 1, TB) if exists(i, c - 1) else 0)
                    if first(i, c):
                        act.wait_ge(layer_zeroed, layer + 1)
                    for b in range(BT):
                        for e in range(2):
                            nc.scalar.copy(
                                vx[layer][e * S:(e + 1) * S].rearrange("p (t b) g c -> p t b g c", b=BT)[:, :, b, :, e * DK:(e + 1) * DK],
                                src[b * S:(b + 1) * S].rearrange("p (t g e d) -> p t g e d", t=TB, g=HP, e=2)[:, :, :, e, :]
                            ).then_inc(done[kind], 1)
                elif kind == "attT":
                    after(act, ready["proj"], mine - 1)
                    nc.scalar.activation(attT[:], src[:], ACT.Identity, bias=column(VB)).then_inc(done[kind], 1)
                    if layer == 2:
                        act.wait_ge(done[kind], mine)
                        if first(i, c):
                            act.wait_ge(setup_pool, KEEP_DONE)
                        nc.scalar.copy(attT[:].rearrange("p (b q) -> p b q", b=BB)[:, :, 0:1],
                                       zeros[:, 0:BB].unsqueeze(2)).then_inc(padded, 1)
                elif kind in NORMED:
                    n = norm_no(i, layer, c, 1 + NORMED.index(kind))
                    after(act, ready["var"], n)
                    nc.scalar.activation(square[:], src[:], ACT.Square,
                                         bias=column(OB if kind == "proj" else BF2)).then_inc(square_done, 1)
                elif kind == "var":
                    after(act, scaled, mine - 1)
                    nc.scalar.activation(rstd[:], src[:], ACT.Ln, bias=eps_ln).then_inc(done[kind], 1)
                elif kind == "ff1":
                    after(act, ready["ff2"], ffn_no(i, layer, c))
                    if first(i, c):
                        act.wait_ge(mask_ready, BT * L)
                    nc.scalar.activation(hT[:, chunk], src[:], ACT.Relu, bias=b1c[:, layer, chunk:chunk + 1]).then_inc(done[kind], 1)
                elif kind == "out":
                    after(act, stored, line(i, 16, 16 * c))
                    nc.scalar.copy(outb[:].rearrange("p t d -> p (t d)"), src[:]).then_inc(done[kind], 1)

            def inverse_deviation(i, layer, c, which):
                n = norm_no(i, layer, c, which)
                act.wait_ge(done["var"], n + 1)
                nc.scalar.activation(rstd[:], rstd[:], ACT.Exp, scale=-0.5).then_inc(rstd_done, 1)

            def stage(i, r, lag, work):
                layer, c, t = at_step(r - lag)
                if exists(i, c):
                    work(i, layer, c, t)

            def jobs(i, part):
                for one_job in jobs_in(part, 1):
                    if exists(i, one_job[3]):
                        job(i, *one_job)

            def norms(i, part):
                for _, kind, layer, c, which in jobs_in(part, 1):
                    if kind == "var" and exists(i, c):
                        inverse_deviation(i, layer, c, which)

            def step(i, r):
                stage(i, r, 2, roots)
                stage(i, r, 1, keep_raw)
                jobs(i, PARTS * r)
                stage(i, r, 2, decays)
                norms(i, PARTS * r)
                jobs(i, PARTS * r + 1)
                norms(i, PARTS * r + 1)
                stage(i, r, 3, probs)
                stage(i, r, 0, exp1)
                jobs(i, PARTS * r + 2)
                stage(i, r, 1, logs)
                norms(i, PARTS * r + 2)

            rounds(act, step)

        @block.vector
        def _(dve):
            count = [0]

            def setup(ins):
                count[0] += 1
                ins.then_inc(setup_dve, 1)
                dve.wait_ge(setup_dve, count[0])

            def zero(n):
                setup(nc.vector.memset(vx[n][:].rearrange("p b g c -> p (b g c)"), 0.0))
                for e in range(2):
                    setup(nc.vector.memset(vx[n][e * S:(e + 1) * S, :, :, 2 * DK + e:2 * DK + e + 1], 1.0))
                nc.vector.memset(kx[n][:].rearrange("p h t -> p (h t)"), 0.0).then_inc(layer_zeroed, 1)

            setup(nc.vector.memset(hidden[:, 0:S], 0.0))
            for t in range(TB):
                setup(nc.vector.memset(E[t][:, H * S:H * S + 1], 0.0))
            dve.wait_ge(setup_act, 1)
            setup(nc.vector.tensor_tensor(al[:], al[:], ge[:], ALU.subtract))
            setup(nc.vector.tensor_tensor(hidden[:, S:SKEW], al[:, :, 0], al[:, :, 1], ALU.is_ge))
            setup(nc.vector.tensor_scalar(hidden[:], hidden[:], NEG, None, ALU.mult))
            assert count[0] == MASK_ROWS, count[0]
            zero(0)
            dve.wait_ge(setup_act, 4)
            setup(nc.vector.scalar_tensor_tensor(gam[:, 4, :], gam[:, 0, :], 0.0, gam[:, 3, :], ALU.max, ALU.add))
            setup(nc.vector.tensor_tensor(gam[:, 4, :], gam[:, 4, :], gam[:, 4, :], ALU.mult))
            dve.wait_ge(setup_pool, CENTRE_DONE)
            for l in range(L):
                setup(nc.vector.tensor_tensor(per_head(decay[:, l]), per_head(dist_ij[:]),
                                              over_keys(gam[:, 4, l * H:(l + 1) * H]), ALU.mult))
            zero(1)
            dve.wait_ge(wT_done, WEIGHTS_DONE)
            zero(2)
            assert count[0] == SETUP_DVE, count[0]
            dve.wait_ge(setup_pool, KEEP_DONE)

            def over(n, k):
                return n * 3 + k

            def max1(i, layer, c, t):
                dve.wait_ge(scores_ready, tile_no(i, layer, c, t) + 1)
                nc.vector.tensor_reduce(neg1[:, t], per_head(psS[t % 2][:]), AX_X, ALU.max, negate=True).then_inc(max1_done, 1)

            def shift1(i, layer, c, t):
                n = tile_no(i, layer, c, t)
                dve.wait_ge(max1_done, n + 1)
                after(dve, tree_step, over(n - TB, 1))
                nc.vector.tensor_tensor(per_head(E[t][:, 0:H * S]), per_head(psS[t % 2][:]), over_keys(neg1[:, t]),
                                        ALU.add).then_inc(shift1_done, 1)

            def scan(i, layer, c, t):
                n = tile_no(i, layer, c, t)
                dve.wait_ge(exp1_done, n + 1)
                after(dve, logitsT_ready, n + 1 - TB)
                nc.vector.tensor_tensor_scan(W[t][:, ::-1], E[t][:, 1:H * S + 1][:, ::-1], keep[:, BMASK[layer]][:, ::-1],
                                             0.0, ALU.add, ALU.mult).then_inc(scan_done, 1)

            def den1_of(i, layer, c, t):
                dve.wait_ge(tree_step, over(tile_no(i, layer, c, t), 3))
                nc.vector.tensor_reduce(den1[:, t], tree[2][:], AX_X, ALU.add).then_inc(den1_done, 1)

            def rden1_of(i, layer, c, t):
                dve.wait_ge(den1_done, tile_no(i, layer, c, t) + 1)
                nc.vector.reciprocal(rden1[:, t], den1[:, t]).then_inc(rden1_done, 1)

            def logits(i, layer, c, t):
                n = tile_no(i, layer, c, t)
                dve.wait_ge(te_done, n + 1)
                dve.wait_ge(raw_done, n + 1)
                nc.vector.scalar_tensor_tensor(W[t][:], W[t][:], TE_MIN, raw[t][:], ALU.max, ALU.mult).then_inc(logits_done, 1)

            def max2(i, layer, c, t):
                dve.wait_ge(logits_done, tile_no(i, layer, c, t) + 1)
                nc.vector.tensor_reduce(neg2[:, t], per_head(W[t][:]), AX_X, ALU.max, negate=True).then_inc(max2_done, 1)

            def shift2(i, layer, c, t):
                dve.wait_ge(max2_done, tile_no(i, layer, c, t) + 1)
                nc.vector.tensor_tensor(per_head(W[t][:]), per_head(W[t][:]), over_keys(neg2[:, t]), ALU.add).then_inc(shift2_done, 1)

            att_parts = psO[:, 0:HP * VW].rearrange("p (g c) -> p g c", g=HP)

            def rden2_of(i, layer, c, t):
                dve.wait_ge(weighted_ready, tile_no(i, layer, c, t) + 1)
                nc.vector.reciprocal(rden2[:, t], att_parts[:, :, 2 * DK:VW]).then_inc(rden2_done, 1)

            def attend(i, layer, c, t):
                dve.wait_ge(rden2_done, tile_no(i, layer, c, t) + 1)
                if t == 0:
                    after(dve, ready["attT"], job_count(i, "attT", layer, c - 1) if exists(i, c - 1) else 0)
                nc.vector.tensor_tensor(att[:, layer, t].rearrange("p (g e d) -> p g e d", g=HP, e=2),
                                        att_parts[:, :, 0:2 * DK].rearrange("p g (e d) -> p g e d", e=2),
                                        rden2[:, t].unsqueeze(3).to_broadcast([P, HP, 2, DK]), ALU.mult).then_inc(att_done, 1)

            def scale(i, place, layer, c, which):
                n = norm_no(i, layer, c, which)
                centred = psJ[BANK[next(m for m, job in enumerate(ORDER) if job[:2] == (NORMED[which - 1], layer))]]
                bias = OB if which == 1 else BF2
                dve.wait_ge(rstd_done, n + 1)
                after(dve, affine_done, n)
                nc.vector.scalar_tensor_tensor(normed[:], centred[:], cols[:, bias, layer:layer + 1], rstd[:],
                                               ALU.add, ALU.mult).then_inc(scaled, 1)

            def stage(i, r, lag, *work):
                layer, c, t = at_step(r - lag)
                if exists(i, c):
                    for one in work:
                        one(i, layer, c, t)

            def affine(i, place, layer, c, which):
                dve.wait_ge(scaled, norm_no(i, layer, c, which) + 1)
                gain, bias = (G1, B1) if which == 1 else (G2, B2)
                if (layer, which) == (1, 1):
                    dst = x1T
                    if exists(i, c - 1):
                        dve.wait_ge(ready["proj"], job_count(i, "proj", 2, c - 1))
                        dve.wait_ge(ready["key"], job_count(i, "key", 2, c - 1))
                elif which == 1:
                    dst = xfT
                    after(dve, ready["ff2"], ffn_no(i, layer, c))
                elif layer == 0:
                    dst = yT
                    if exists(i, c - 1):
                        dve.wait_ge(ready["value"], job_count(i, "value", 2, c - 1))
                else:
                    dst = outT
                    after(dve, ready["out"], line(i, 1, c))
                nc.vector.tensor_scalar(dst[:], normed[:], cols[:, gain, layer:layer + 1], cols[:, bias, layer:layer + 1],
                                        ALU.mult, ALU.add).then_inc(affine_done, 1)

            def norms(i, part, late, work):
                for place, kind, layer, c, which in jobs_in(part, late):
                    if kind == "var" and exists(i, c):
                        work(i, place, layer, c, which)

            def step(i, r):
                stage(i, r, 1, scan)
                stage(i, r, 0, max1)
                stage(i, r, 1, den1_of)
                stage(i, r, 0, shift1)
                stage(i, r, 1, rden1_of)
                norms(i, PARTS * r, 2, scale)
                stage(i, r, 4, rden2_of)
                norms(i, PARTS * r + 1, 2, scale)
                norms(i, PARTS * r, 2, affine)
                norms(i, PARTS * r + 1, 2, affine)
                stage(i, r, 4, attend)
                stage(i, r, 2, logits)
                stage(i, r, 2, max2)
                stage(i, r, 2, shift2)
                norms(i, PARTS * r + 2, 2, scale)
                norms(i, PARTS * r + 2, 2, affine)

            rounds(dve, step)

        @block.gpsimd
        def _(pool):
            count = [0]

            def setup(ins):
                count[0] += 1
                ins.then_inc(setup_pool, 1)
                pool.wait_ge(setup_pool, count[0])

            for n, value in enumerate((TINY, EPS_LOG, 1.0, EPS_LN)):
                last = nc.gpsimd.memset(small[:, n:n + 1], value)
            setup(last)
            setup(nc.gpsimd.memset(identf[:], 0.0))
            setup(nc.gpsimd.affine_select(out=identf[:], in_=identf[:], compare_op=ALU.not_equal, fill=1.0, base=0,
                                          pattern=[[-1, P]], channel_multiplier=1))
            for n in range(BT):
                last = nc.gpsimd.iota(per_head(dist_ij[n * S:(n + 1) * S]), pattern=[[0, H], [-1, S]], base=0,
                                      channel_multiplier=1, allow_small_or_imprecise_dtypes=True)
            setup(last)
            setup(nc.gpsimd.memset(average[:], 1.0 / D))
            setup(nc.gpsimd.tensor_tensor(centre[:], identf[:], average[:], ALU.subtract))
            assert count[0] == CENTRE_DONE, count[0]
            setup(nc.gpsimd.memset(identb[:], 0.0))
            setup(nc.gpsimd.affine_select(out=identb[:], in_=identb[:], compare_op=ALU.not_equal, fill=1.0, base=0,
                                          pattern=[[-1, P]], channel_multiplier=1))
            setup(nc.gpsimd.memset(zeros[:], 0.0))
            for m in range(2):
                for n in range(BT):
                    rows = slice(n * S, (n + 1) * S)
                    setup(nc.gpsimd.affine_select(out=per_head(causal_bias[rows, m]), in_=per_head(zeros[rows]), compare_op=ALU.is_gt,
                                                  fill=NEG, base=m, pattern=[[0, H], [-1, S]], channel_multiplier=1))
                    setup(nc.gpsimd.affine_select(out=per_head(keep[rows, m]), in_=per_head(zeros[rows]), compare_op=ALU.is_ge,
                                                  fill=1.0, base=1 - m, pattern=[[0, H], [1, S]], channel_multiplier=-1))
            for m in range(2):
                setup(nc.gpsimd.memset(per_head(keep[:, m])[:, :, S - 1:S], 0.0))
            assert count[0] == KEEP_DONE, count[0]
            pool.wait_ge(skew_read, 16 * BT)
            for l in range(L):
                for n in range(BT):
                    rows = slice(n * S, (n + 1) * S)
                    nc.gpsimd.affine_select(out=per_head(mask_bias[rows, l]), in_=shifted_mask[rows, l], compare_op=ALU.is_ge,
                                                  fill=0.0, base=-BMASK[l], pattern=[[0, H], [1, S]], channel_multiplier=-1).then_inc(mask_ready, 1)
                    pool.wait_ge(mask_ready, BT * l + n + 1)
            pool.wait_ge(setup_dve, SETUP_DVE)

            def sums(k):
                half = (32, 16, 8)[k]

                def work(i, layer, c, t):
                    n = tile_no(i, layer, c, t)
                    if k == 0:
                        pool.wait_ge(exp1_done, n + 1)
                    after(pool, tree_step, n * 3 + k)
                    if k == 2:
                        after(pool, den1_done, n)
                    src = per_head(E[t][:, 0:H * S]) if k == 0 else tree[k - 1][:]
                    nc.gpsimd.tensor_tensor(tree[k][:], src[:, :, 0:half], src[:, :, half:2 * half], ALU.add).then_inc(tree_step, 1)

                return work

            def decayed(i, layer, c, t):
                n = tile_no(i, layer, c, t)
                pool.wait_ge(scan_done, n + 1)
                nc.gpsimd.tensor_tensor(W[t][:], W[t][:], decay[:, layer], ALU.mult).then_inc(decay_done, 1)

            def distances(i, layer, c, t):
                n = tile_no(i, layer, c, t)
                pool.wait_ge(decay_done, n + 1)
                pool.wait_ge(rden1_done, n + 1)
                nc.gpsimd.tensor_tensor(per_head(W[t][:]), per_head(W[t][:]), over_keys(rden1[:, t]), ALU.mult).then_inc(dist_done, 1)

            def stage(i, r, lag, work):
                layer, c, t = at_step(r - lag)
                if exists(i, c):
                    work(i, layer, c, t)

            def step(i, r):
                stage(i, r, 2, distances)
                stage(i, r, 1, sums(0))
                stage(i, r, 1, sums(1))
                stage(i, r, 1, sums(2))
                stage(i, r, 1, decayed)

            rounds(pool, step)


WEIGHT_LOADS = 3 + 4 + 8 + 1
WEIGHTS_DONE = 10
WT_DONE = WEIGHTS_DONE + 2
MASK_ROWS = 1 + TB + 3
SETUP_DVE = MASK_ROWS + 2 + L + 3 * L
CENTRE_DONE = 6
KEEP_DONE = CENTRE_DONE + 3 + 8 + 2


_INS = ["x", "ctx_1024", "L0_xattn_kW", "L0_xattn_kb", "L0_xattn_vW", "L0_xattn_vb", "L0_xattn_oW", "L0_xattn_ob",
        "L0_xattn_gammas", "L0_xattn_alphas", "L0_xattn_ln1_g", "L0_xattn_ln1_b", "L0_xattn_w1", "L0_xattn_b1",
        "L0_xattn_w2", "L0_xattn_b2", "L0_xattn_ln2_g", "L0_xattn_ln2_b", "L0_xattn_gumbel_E"]


def kernel(**inputs):
    import numpy as _np
    import concourse.bacc as _bacc
    from concourse import mybir as _mybir
    from concourse.bass_utils import run_bass_kernel_spmd as _run

    nc = _bacc.Bacc("TRN2", target_bir_lowering=False, num_devices=1)
    arrays, args = {}, []
    for name in _INS:
        a = _np.ascontiguousarray(inputs[name])
        arrays[f"in_{name}"] = a
        args.append(nc.dram_tensor(f"in_{name}", a.shape, _mybir.dt.from_np(a.dtype), kind="ExternalInput").ap())
    out = nc.dram_tensor("out_0", (B, S, D), F32, kind="ExternalOutput").ap()
    build(nc, *args, out)
    r = _run(nc, [arrays], core_ids=[0])
    return r.results[0]["out_0"]
```
